# Optimizing a Trainium2 kernel written in Bass

```python
import numpy as np
import jax
import jax.numpy as jnp

def _softmax(x, axis=-1):
    return jax.nn.softmax(x, axis=axis)

def _gelu(x):
    return jax.nn.gelu(x, approximate=True)

def _silu(x):
    return jax.nn.silu(x)

def _sigmoid(x):
    return jax.nn.sigmoid(x)

def _layernorm(x, axis=-1, eps=1e-05):
    m = jnp.mean(x, axis=axis, keepdims=True)
    v = jnp.var(x, axis=axis, keepdims=True)
    return (x - m) / jnp.sqrt(v + eps)

def _scatter_add(tgt, idx, src, axis=0):
    return tgt.at[idx].add(src)

def _segment_sum(src, seg, n):
    return jax.ops.segment_sum(src, seg, n)
kernel_name = 'mk_conv_preact_d4_conv_nhwc128_r2_e324a9'

def setup_inputs(seed: int=0):
    np.random.seed(seed)
    _w = jnp.asarray

    def _rec_inputs():
        import jax
        import jax.numpy as jnp
        _gk = jax.random.key(seed)
        x = -0.000125 + 0.9999 * jax.random.normal(jax.random.fold_in(_gk, 1), (1, 256, 256, 64), jnp.float32)
        return x
    x = _rec_inputs()

    def _L0_conv_setup():
        import jax, jax.numpy as jnp
        import numpy as np
        B, L, DIM, HID = (1, 256, 64, 64)
        EPS = 1e-05

        def layernorm(x, w, b):
            mu = jnp.mean(x, axis=-1, keepdims=True)
            var = jnp.var(x, axis=-1, keepdims=True)
            return (x - mu) * jax.lax.rsqrt(var + EPS) * w + b
        key = jax.random.key(seed)
        ks = jax.random.split(key, 12)
        s = 1.0 / np.sqrt(DIM)
        sh = 1.0 / np.sqrt(HID)
        x = jax.random.normal(ks[0], (B, L, L, DIM), dtype=jnp.float32)
        mask = (jax.random.uniform(ks[1], (B, L, L)) > 0.1).astype(jnp.float32)
        return {'x': x, 'mask': mask, 'norm_w': jnp.ones((DIM,), jnp.float32), 'norm_b': jnp.zeros((DIM,), jnp.float32), 'w_left': jax.random.uniform(ks[2], (HID, DIM), jnp.float32, -s, s), 'w_right': jax.random.uniform(ks[3], (HID, DIM), jnp.float32, -s, s), 'w_lgate': jax.random.uniform(ks[4], (HID, DIM), jnp.float32, -s, s), 'w_rgate': jax.random.uniform(ks[5], (HID, DIM), jnp.float32, -s, s), 'w_ogate': jax.random.uniform(ks[6], (HID, DIM), jnp.float32, -s, s), 'onorm_w': jnp.ones((HID,), jnp.float32), 'onorm_b': jnp.zeros((HID,), jnp.float32), 'w_out': jax.random.uniform(ks[7], (DIM, HID), jnp.float32, -sh, sh)}
    _L0_conv_all = _L0_conv_setup()
    _L0_conv_in = {k: v for k, v in _L0_conv_all.items() if k in ('mask', 'norm_w', 'norm_b', 'w_left', 'w_right', 'w_lgate', 'w_rgate', 'w_ogate', 'onorm_w', 'onorm_b', 'w_out')}
    del _L0_conv_all

    def _L1_conv_setup():
        import jax, jax.numpy as jnp
        import numpy as np
        EPS = 1e-05

        def layer_norm(x, a, b):
            m = jnp.mean(x, axis=-1, keepdims=True)
            v = jnp.var(x, axis=-1, keepdims=True)
            return a * (x - m) / jnp.sqrt(v + EPS) + b
        key = jax.random.key(seed)
        ks = jax.random.split(key, 16)
        b, n, d, h = (1, 192, 64, 64)
        s = 1.0 / np.sqrt(d)
        inp = {'x': jax.random.normal(ks[0], (b, n, n, d), dtype=jnp.float32), 'norm_a': jnp.ones((d,), jnp.float32), 'norm_b': jnp.zeros((d,), jnp.float32), 'Wl': jax.random.normal(ks[1], (d, h), jnp.float32) * s, 'bl': jnp.zeros((h,), jnp.float32), 'Wr': jax.random.normal(ks[2], (d, h), jnp.float32) * s, 'br': jnp.zeros((h,), jnp.float32), 'Wlg': jax.random.normal(ks[3], (d, h), jnp.float32) * s, 'blg': jnp.ones((h,), jnp.float32), 'Wrg': jax.random.normal(ks[4], (d, h), jnp.float32) * s, 'brg': jnp.ones((h,), jnp.float32), 'Wog': jax.random.normal(ks[5], (d, h), jnp.float32) * s, 'bog': jnp.ones((h,), jnp.float32), 'on_a': jnp.ones((h,), jnp.float32), 'on_b': jnp.zeros((h,), jnp.float32), 'Wo': jax.random.normal(ks[6], (h, d), jnp.float32) * s, 'bo': jnp.zeros((d,), jnp.float32)}
        return inp
    _L1_conv_all = _L1_conv_setup()
    _L1_conv_in = {k: v for k, v in _L1_conv_all.items() if k in ('norm_a', 'norm_b', 'Wl', 'bl', 'Wr', 'br', 'Wlg', 'blg', 'Wrg', 'brg', 'Wog', 'bog', 'on_a', 'on_b', 'Wo', 'bo')}
    del _L1_conv_all

    def _L2_conv_setup():
        import jax, jax.numpy as jnp
        import numpy as np
        LN_EPS = 1e-05

        def _layer_norm(x, scale, bias):
            mu = jnp.mean(x, axis=-1, keepdims=True)
            var = jnp.mean(jnp.square(x - mu), axis=-1, keepdims=True)
            return (x - mu) * jax.lax.rsqrt(var + LN_EPS) * scale + bias
        key = jax.random.key(seed)
        B, N, C_Z, C_H = (1, 256, 64, 64)
        ks = jax.random.split(key, 8)
        s = 1.0 / np.sqrt(C_Z)
        inp = {'z': jax.random.normal(ks[0], (B, N, N, C_Z), dtype=jnp.float32), 'mask': jnp.ones((B, N, N), dtype=jnp.float32), 'w_a_p': jax.random.normal(ks[1], (C_Z, C_H), dtype=jnp.float32) * s, 'b_a_p': jnp.zeros((C_H,), dtype=jnp.float32), 'w_a_g': jnp.zeros((C_Z, C_H), dtype=jnp.float32), 'b_a_g': jnp.ones((C_H,), dtype=jnp.float32), 'w_b_p': jax.random.normal(ks[2], (C_Z, C_H), dtype=jnp.float32) * s, 'b_b_p': jnp.zeros((C_H,), dtype=jnp.float32), 'w_b_g': jnp.zeros((C_Z, C_H), dtype=jnp.float32), 'b_b_g': jnp.ones((C_H,), dtype=jnp.float32), 'w_g': jnp.zeros((C_Z, C_Z), dtype=jnp.float32), 'b_g': jnp.ones((C_Z,), dtype=jnp.float32), 'w_z': jax.random.normal(ks[3], (C_H, C_Z), dtype=jnp.float32) * (1.0 / np.sqrt(C_H)), 'b_z': jnp.zeros((C_Z,), dtype=jnp.float32), 'ln_in_scale': jnp.ones((C_Z,), dtype=jnp.float32), 'ln_in_bias': jnp.zeros((C_Z,), dtype=jnp.float32), 'ln_out_scale': jnp.ones((C_H,), dtype=jnp.float32), 'ln_out_bias': jnp.zeros((C_H,), dtype=jnp.float32)}
        return inp
    _L2_conv_all = _L2_conv_setup()
    _L2_conv_in = {k: v for k, v in _L2_conv_all.items() if k in ('mask', 'w_a_p', 'b_a_p', 'w_a_g', 'b_a_g', 'w_b_p', 'b_b_p', 'w_b_g', 'b_b_g', 'w_g', 'b_g', 'w_z', 'b_z', 'ln_in_scale', 'ln_in_bias', 'ln_out_scale', 'ln_out_bias')}
    del _L2_conv_all

    def _L3_conv_setup():
        import jax, jax.numpy as jnp
        import numpy as np
        B, N, D, C = (1, 256, 64, 64)
        EPS = 1e-05

        def _layernorm(x, g, b):
            m = jnp.mean(x, axis=-1, keepdims=True)
            v = jnp.mean(jnp.square(x - m), axis=-1, keepdims=True)
            return (x - m) * jax.lax.rsqrt(v + EPS) * g + b
        key = jax.random.key(seed)
        ks = jax.random.split(key, 14)
        sD = 1.0 / np.sqrt(D)
        sC = 1.0 / np.sqrt(C)

        def w(k, shape, scale):
            return jax.random.normal(k, shape, dtype=jnp.float32) * scale
        return {'x': jax.random.normal(ks[0], (B, N, N, D), dtype=jnp.float32), 'ln_in_g': jnp.ones((D,), jnp.float32), 'ln_in_b': jnp.zeros((D,), jnp.float32), 'ln_out_g': jnp.ones((C,), jnp.float32), 'ln_out_b': jnp.zeros((C,), jnp.float32), 'Wl': w(ks[1], (D, C), sD), 'bl': w(ks[2], (C,), 0.02), 'Wr': w(ks[3], (D, C), sD), 'br': w(ks[4], (C,), 0.02), 'Wo': w(ks[5], (C, D), sC), 'bo': w(ks[6], (D,), 0.02), 'Wlg': w(ks[7], (D, C), sD), 'blg': w(ks[8], (C,), 0.02), 'Wrg': w(ks[9], (D, C), sD), 'brg': w(ks[10], (C,), 0.02), 'Wog': w(ks[11], (D, D), sD), 'bog': w(ks[12], (D,), 0.02)}
    _L3_conv_all = _L3_conv_setup()
    _L3_conv_in = {k: v for k, v in _L3_conv_all.items() if k in ('ln_in_g', 'ln_in_b', 'ln_out_g', 'ln_out_b', 'Wl', 'bl', 'Wr', 'br', 'Wo', 'bo', 'Wlg', 'blg', 'Wrg', 'brg', 'Wog', 'bog')}
    del _L3_conv_all
    return {'x': x, 'L0_conv_mask': _L0_conv_in['mask'], 'L0_conv_norm_w': _L0_conv_in['norm_w'], 'L0_conv_norm_b': _L0_conv_in['norm_b'], 'L0_conv_w_left': _L0_conv_in['w_left'], 'L0_conv_w_right': _L0_conv_in['w_right'], 'L0_conv_w_lgate': _L0_conv_in['w_lgate'], 'L0_conv_w_rgate': _L0_conv_in['w_rgate'], 'L0_conv_w_ogate': _L0_conv_in['w_ogate'], 'L0_conv_onorm_w': _L0_conv_in['onorm_w'], 'L0_conv_onorm_b': _L0_conv_in['onorm_b'], 'L0_conv_w_out': _L0_conv_in['w_out'], 'L1_conv_norm_a': _L1_conv_in['norm_a'], 'L1_conv_norm_b': _L1_conv_in['norm_b'], 'L1_conv_Wl': _L1_conv_in['Wl'], 'L1_conv_bl': _L1_conv_in['bl'], 'L1_conv_Wr': _L1_conv_in['Wr'], 'L1_conv_br': _L1_conv_in['br'], 'L1_conv_Wlg': _L1_conv_in['Wlg'], 'L1_conv_blg': _L1_conv_in['blg'], 'L1_conv_Wrg': _L1_conv_in['Wrg'], 'L1_conv_brg': _L1_conv_in['brg'], 'L1_conv_Wog': _L1_conv_in['Wog'], 'L1_conv_bog': _L1_conv_in['bog'], 'L1_conv_on_a': _L1_conv_in['on_a'], 'L1_conv_on_b': _L1_conv_in['on_b'], 'L1_conv_Wo': _L1_conv_in['Wo'], 'L1_conv_bo': _L1_conv_in['bo'], 'L2_conv_mask': _L2_conv_in['mask'], 'L2_conv_w_a_p': _L2_conv_in['w_a_p'], 'L2_conv_b_a_p': _L2_conv_in['b_a_p'], 'L2_conv_w_a_g': _L2_conv_in['w_a_g'], 'L2_conv_b_a_g': _L2_conv_in['b_a_g'], 'L2_conv_w_b_p': _L2_conv_in['w_b_p'], 'L2_conv_b_b_p': _L2_conv_in['b_b_p'], 'L2_conv_w_b_g': _L2_conv_in['w_b_g'], 'L2_conv_b_b_g': _L2_conv_in['b_b_g'], 'L2_conv_w_g': _L2_conv_in['w_g'], 'L2_conv_b_g': _L2_conv_in['b_g'], 'L2_conv_w_z': _L2_conv_in['w_z'], 'L2_conv_b_z': _L2_conv_in['b_z'], 'L2_conv_ln_in_scale': _L2_conv_in['ln_in_scale'], 'L2_conv_ln_in_bias': _L2_conv_in['ln_in_bias'], 'L2_conv_ln_out_scale': _L2_conv_in['ln_out_scale'], 'L2_conv_ln_out_bias': _L2_conv_in['ln_out_bias'], 'L3_conv_ln_in_g': _L3_conv_in['ln_in_g'], 'L3_conv_ln_in_b': _L3_conv_in['ln_in_b'], 'L3_conv_ln_out_g': _L3_conv_in['ln_out_g'], 'L3_conv_ln_out_b': _L3_conv_in['ln_out_b'], 'L3_conv_Wl': _L3_conv_in['Wl'], 'L3_conv_bl': _L3_conv_in['bl'], 'L3_conv_Wr': _L3_conv_in['Wr'], 'L3_conv_br': _L3_conv_in['br'], 'L3_conv_Wo': _L3_conv_in['Wo'], 'L3_conv_bo': _L3_conv_in['bo'], 'L3_conv_Wlg': _L3_conv_in['Wlg'], 'L3_conv_blg': _L3_conv_in['blg'], 'L3_conv_Wrg': _L3_conv_in['Wrg'], 'L3_conv_brg': _L3_conv_in['brg'], 'L3_conv_Wog': _L3_conv_in['Wog'], 'L3_conv_bog': _L3_conv_in['bog']}

def reference(x, L0_conv_mask, L0_conv_norm_w, L0_conv_norm_b, L0_conv_w_left, L0_conv_w_right, L0_conv_w_lgate, L0_conv_w_rgate, L0_conv_w_ogate, L0_conv_onorm_w, L0_conv_onorm_b, L0_conv_w_out, L1_conv_norm_a, L1_conv_norm_b, L1_conv_Wl, L1_conv_bl, L1_conv_Wr, L1_conv_br, L1_conv_Wlg, L1_conv_blg, L1_conv_Wrg, L1_conv_brg, L1_conv_Wog, L1_conv_bog, L1_conv_on_a, L1_conv_on_b, L1_conv_Wo, L1_conv_bo, L2_conv_mask, L2_conv_w_a_p, L2_conv_b_a_p, L2_conv_w_a_g, L2_conv_b_a_g, L2_conv_w_b_p, L2_conv_b_b_p, L2_conv_w_b_g, L2_conv_b_b_g, L2_conv_w_g, L2_conv_b_g, L2_conv_w_z, L2_conv_b_z, L2_conv_ln_in_scale, L2_conv_ln_in_bias, L2_conv_ln_out_scale, L2_conv_ln_out_bias, L3_conv_ln_in_g, L3_conv_ln_in_b, L3_conv_ln_out_g, L3_conv_ln_out_b, L3_conv_Wl, L3_conv_bl, L3_conv_Wr, L3_conv_br, L3_conv_Wo, L3_conv_bo, L3_conv_Wlg, L3_conv_blg, L3_conv_Wrg, L3_conv_brg, L3_conv_Wog, L3_conv_bog):
    import jax
    import jax.numpy as jnp

    def _L0_conv_ref(x, mask, norm_w, norm_b, w_left, w_right, w_lgate, w_rgate, w_ogate, onorm_w, onorm_b, w_out):
        import jax, jax.numpy as jnp
        import numpy as np
        B, L, DIM, HID = (1, 256, 64, 64)
        EPS = 1e-05

        def layernorm(x, w, b):
            mu = jnp.mean(x, axis=-1, keepdims=True)
            var = jnp.var(x, axis=-1, keepdims=True)
            return (x - mu) * jax.lax.rsqrt(var + EPS) * w + b
        xn = layernorm(x, norm_w, norm_b)
        m = mask[..., None]
        left = jnp.einsum('bijd,hd->bijh', xn, w_left) * m
        right = jnp.einsum('bijd,hd->bijh', xn, w_right) * m
        lg = jax.nn.sigmoid(jnp.einsum('bijd,hd->bijh', xn, w_lgate))
        rg = jax.nn.sigmoid(jnp.einsum('bijd,hd->bijh', xn, w_rgate))
        og = jax.nn.sigmoid(jnp.einsum('bijd,hd->bijh', xn, w_ogate))
        left = (left * lg).astype(jnp.bfloat16)
        right = (right * rg).astype(jnp.bfloat16)
        out = jnp.einsum('bikh,bjkh->bijh', left, right).astype(jnp.float32)
        out = layernorm(out, onorm_w, onorm_b) * og
        return jnp.einsum('bijh,dh->bijd', out, w_out)

    def _L1_conv_ref(x, norm_a, norm_b, Wl, bl, Wr, br, Wlg, blg, Wrg, brg, Wog, bog, on_a, on_b, Wo, bo):
        import jax, jax.numpy as jnp
        import numpy as np
        EPS = 1e-05

        def layer_norm(x, a, b):
            m = jnp.mean(x, axis=-1, keepdims=True)
            v = jnp.var(x, axis=-1, keepdims=True)
            return a * (x - m) / jnp.sqrt(v + EPS) + b
        n = x.shape[1]
        xn = layer_norm(x, norm_a, norm_b)
        left = (xn @ Wl + bl) * jax.nn.sigmoid(xn @ Wlg + blg)
        right = (xn @ Wr + br) * jax.nn.sigmoid(xn @ Wrg + brg)
        out_gate = jax.nn.sigmoid(xn @ Wog + bog)
        out = jnp.einsum('bkjd,bkid->bijd', left.astype(jnp.float32), right.astype(jnp.float32)) / n
        out = out.astype(x.dtype)
        out = layer_norm(out, on_a, on_b) * out_gate
        return out @ Wo + bo

    def _L2_conv_ref(z, mask, w_a_p, b_a_p, w_a_g, b_a_g, w_b_p, b_b_p, w_b_g, b_b_g, w_g, b_g, w_z, b_z, ln_in_scale, ln_in_bias, ln_out_scale, ln_out_bias):
        import jax, jax.numpy as jnp
        import numpy as np
        LN_EPS = 1e-05

        def _layer_norm(x, scale, bias):
            mu = jnp.mean(x, axis=-1, keepdims=True)
            var = jnp.mean(jnp.square(x - mu), axis=-1, keepdims=True)
            return (x - mu) * jax.lax.rsqrt(var + LN_EPS) * scale + bias
        z = _layer_norm(z, ln_in_scale, ln_in_bias)
        m = mask[..., None]
        a = jax.nn.sigmoid(z @ w_a_g + b_a_g) * m * (z @ w_a_p + b_a_p)
        b = jax.nn.sigmoid(z @ w_b_g + b_b_g) * m * (z @ w_b_p + b_b_p)
        x = jnp.einsum('bikc,bjkc->bijc', a, b)
        x = _layer_norm(x, ln_out_scale, ln_out_bias)
        x = x @ w_z + b_z
        g = jax.nn.sigmoid(z @ w_g + b_g)
        return x * g

    def _L3_conv_ref(x, ln_in_g, ln_in_b, ln_out_g, ln_out_b, Wl, bl, Wr, br, Wo, bo, Wlg, blg, Wrg, brg, Wog, bog):
        import jax, jax.numpy as jnp
        import numpy as np
        B, N, D, C = (1, 256, 64, 64)
        EPS = 1e-05

        def _layernorm(x, g, b):
            m = jnp.mean(x, axis=-1, keepdims=True)
            v = jnp.mean(jnp.square(x - m), axis=-1, keepdims=True)
            return (x - m) * jax.lax.rsqrt(v + EPS) * g + b
        xn = _layernorm(x, ln_in_g, ln_in_b)
        left = jax.nn.sigmoid(xn @ Wlg + blg) * (xn @ Wl + bl)
        right = jax.nn.sigmoid(xn @ Wrg + brg) * (xn @ Wr + br)
        out = jnp.einsum('bkic,bkjc->bijc', left, right)
        out = jax.nn.sigmoid(xn @ Wog + bog) * (_layernorm(out, ln_out_g, ln_out_b) @ Wo + bo)
        return out

    def _gn(v, G=32, eps=1e-05):
        B_, H_, W_, C_ = v.shape
        g = v.reshape(B_, H_, W_, G, C_ // G)
        m = jnp.mean(g, axis=(1, 2, 4), keepdims=True)
        s = jnp.var(g, axis=(1, 2, 4), keepdims=True)
        return ((g - m) / jnp.sqrt(s + eps)).reshape(v.shape)

    def _ln_c(v, eps=1e-06):
        m = jnp.mean(v, axis=-1, keepdims=True)
        s = jnp.var(v, axis=-1, keepdims=True)
        return (v - m) / jnp.sqrt(s + eps)

    def _ln_t(v, eps=1e-05):
        m = jnp.mean(v, axis=-1, keepdims=True)
        s = jnp.var(v, axis=-1, keepdims=True)
        return (v - m) / jnp.sqrt(s + eps)

    def _to_tokens(v):
        B_, H_, W_, C_ = v.shape
        return v.reshape(B_, H_ * W_, C_)

    def _from_tokens(t, like):
        return t.reshape(like.shape)
    x = x + _L0_conv_ref(_gn(x), L0_conv_mask, L0_conv_norm_w, L0_conv_norm_b, L0_conv_w_left, L0_conv_w_right, L0_conv_w_lgate, L0_conv_w_rgate, L0_conv_w_ogate, L0_conv_onorm_w, L0_conv_onorm_b, L0_conv_w_out)
    x = x + _L1_conv_ref(_gn(x), L1_conv_norm_a, L1_conv_norm_b, L1_conv_Wl, L1_conv_bl, L1_conv_Wr, L1_conv_br, L1_conv_Wlg, L1_conv_blg, L1_conv_Wrg, L1_conv_brg, L1_conv_Wog, L1_conv_bog, L1_conv_on_a, L1_conv_on_b, L1_conv_Wo, L1_conv_bo)
    x = x + _L2_conv_ref(_gn(x), L2_conv_mask, L2_conv_w_a_p, L2_conv_b_a_p, L2_conv_w_a_g, L2_conv_b_a_g, L2_conv_w_b_p, L2_conv_b_b_p, L2_conv_w_b_g, L2_conv_b_b_g, L2_conv_w_g, L2_conv_b_g, L2_conv_w_z, L2_conv_b_z, L2_conv_ln_in_scale, L2_conv_ln_in_bias, L2_conv_ln_out_scale, L2_conv_ln_out_bias)
    x = x + _L3_conv_ref(_gn(x), L3_conv_ln_in_g, L3_conv_ln_in_b, L3_conv_ln_out_g, L3_conv_ln_out_b, L3_conv_Wl, L3_conv_bl, L3_conv_Wr, L3_conv_br, L3_conv_Wo, L3_conv_bo, L3_conv_Wlg, L3_conv_blg, L3_conv_Wrg, L3_conv_brg, L3_conv_Wog, L3_conv_bog)
    return x

_drawn_inputs = setup_inputs


def setup_inputs(seed=0):
    import zlib

    import numpy as np

    out = dict(_drawn_inputs(seed))
    spreads = {'L0_conv_norm_w': (1.0, 0.2),
     'L0_conv_norm_b': (0.0, 0.1),
     'L0_conv_onorm_w': (1.0, 0.2),
     'L0_conv_onorm_b': (0.0, 0.1),
     'L1_conv_norm_a': (1.0, 0.2),
     'L1_conv_norm_b': (0.0, 0.1),
     'L1_conv_bl': (0.0, 0.1),
     'L1_conv_br': (0.0, 0.1),
     'L1_conv_blg': (1.0, 0.2),
     'L1_conv_brg': (1.0, 0.2),
     'L1_conv_bog': (1.0, 0.2),
     'L1_conv_on_a': (1.0, 0.2),
     'L1_conv_on_b': (0.0, 0.1),
     'L1_conv_bo': (0.0, 0.1),
     'L2_conv_b_a_p': (0.0, 0.1),
     'L2_conv_w_a_g': (0.0, 0.1),
     'L2_conv_b_a_g': (1.0, 0.6),
     'L2_conv_b_b_p': (0.0, 0.1),
     'L2_conv_w_b_g': (0.0, 0.1),
     'L2_conv_b_b_g': (1.0, 0.584),
     'L2_conv_w_g': (0.0, 0.1),
     'L2_conv_b_g': (1.0, 0.6),
     'L2_conv_b_z': (0.0, 0.1),
     'L2_conv_ln_in_scale': (1.0, 0.2),
     'L2_conv_ln_in_bias': (0.0, 0.1),
     'L2_conv_ln_out_scale': (1.0, 0.2),
     'L2_conv_ln_out_bias': (0.0, 0.1),
     'L3_conv_ln_in_g': (1.0, 0.2),
     'L3_conv_ln_in_b': (0.0, 0.1),
     'L3_conv_ln_out_g': (1.0, 0.2),
     'L3_conv_ln_out_b': (0.0, 0.1)}
    factors = {'L3_conv_bl': 3.322,
     'L3_conv_br': 2.876,
     'L3_conv_bo': 7.459,
     'L3_conv_blg': 8.0,
     'L3_conv_brg': 8.0,
     'L3_conv_bog': 22.051}
    for name, (base, spread) in spreads.items():
        noise = np.random.default_rng([zlib.crc32(name.encode()), seed]).standard_normal(out[name].shape)
        drawn = base * np.exp(spread * noise) if base else spread * noise
        out[name] = jnp.asarray(drawn.astype(out[name].dtype))
    for name, factor in factors.items():
        out[name] = (out[name] * factor).astype(out[name].dtype)
    return out
```

```python
from contextlib import ExitStack

import concourse.bass as bass
from concourse import mybir

F32 = mybir.dt.float32
BF16 = mybir.dt.bfloat16
ALU = mybir.AluOpType
ACT = mybir.ActivationFunctionType

P = 128
N = 256
C = 64
HALF = 32
NT = N // P
BLK = 16
COLS = 2048
NCH = N * N // 2 // COLS
BANK = 512
EPS = 1e-5
GW = 2 * BANK
CREDIT = 64

LAYERS = [
    dict(k_is_b=True, masked=True, low=True, left_a=True, gate_first=True, div=1.0),
    dict(k_is_b=False, masked=False, low=False, left_a=False, gate_first=True, div=float(N)),
    dict(k_is_b=True, masked=True, low=False, left_a=True, gate_first=False, div=1.0),
    dict(k_is_b=False, masked=False, low=False, left_a=True, gate_first=False, div=1.0),
]

K_CENTER, K_MEAN, K_GROUP, K_IDENT, K_DROP, K_FIRST, K_END = 0, 128, 256, 384, 512, 640, 768
W_CAT, W_BIAS, W_OUT, W_VEC, W_END = 0, 320, 640, 768, 773
V_NW, V_NB, V_OW, V_OB, V_BO = range(5)


class Sem:

    def __init__(self, handle):
        self.s, self.n = handle, CREDIT

    def past(self, n):
        return self.base + n


def build(nc, x_in, masks, consts, params, out):
    ctx = ExitStack()
    with ctx:
        def sb(name, shape, dt=F32):
            return ctx.enter_context(nc.sbuf_tensor(name, shape, dt))

        sems = []

        def sem(name):
            s = Sem(ctx.enter_context(nc.semaphore(name)))
            sems.append(s)
            return s

        XT = nc.dram_tensor("XT", [NCH, P, COLS], F32).ap()
        XH = nc.dram_tensor("XH", [NCH, P, COLS], F32).ap()
        XHA = XH.rearrange("n p f -> (n p f)").rearrange("(p f) -> p f", p=P)
        OS = nc.dram_tensor("OS", [NT, N // 16, 4, P, 256], F32).ap()
        OSL = nc.dram_tensor("OSL", [NT, N // 16, 4, P, 256], BF16).ap()

        LR = sb("LR", [P, NT, C, N])
        LRb = LR[:, :, :, :].rearrange("p t c m -> p (t c m)").bitcast(BF16)[:, 0:NT * C * N] \
            .rearrange("p (t c m) -> p t c m", t=NT, c=C)
        flat = LR[:, :, :, :].rearrange("p t c m -> p (t c m)")

        class Arena:

            def __init__(self):
                self.at = 0

            def take(self, cols):
                v = flat[:, self.at:self.at + cols]
                self.at += cols
                assert self.at <= NT * C * N
                return v

        obuf = [sb(f"obuf{i}", [P, 16 * 256]) for i in range(2)]
        xh_b = [o[:, 0:COLS] for o in obuf]
        sig = [sb(f"sig{i}", [P, C, 8]) for i in range(2)]
        msg = [sb(f"msg{i}", [P, C, 8]) for i in range(2)]
        squares = [sb(f"squares{i}", [P, 4 * N]) for i in range(2)]
        sum1 = sb("sum1", [P, NT, 2 * N])
        sum2 = sb("sum2", [P, NT, 2 * N])
        mask_sb = sb("mask_sb", [P, NT, N])
        kst = sb("kst", [P, K_END])
        prm = sb("prm", [P, W_END])
        wfold = sb("wfold", [C, 320])
        bfirst = sb("bfirst", [C, P])
        wproj = sb("wproj", [P, 320])
        wog = sb("wog", [P, P])
        cen = sb("cen", [P, P])
        small = sb("small", [P, 16])
        stats = sb("stats", [P, 4 * NCH, 6])
        eps1 = sb("eps1", [P, 1])
        epso = sb("epso", [P, 1])

        banks = [ctx.enter_context(nc.psum_tensor(f"bank{i}", [P, GW], F32)) for i in range(4)]

        def bank(i):
            return banks[i // 2][:, (i % 2) * BANK:(i % 2 + 1) * BANK]

        loaded = [sem(f"loaded{i}") for i in range(2)]
        loaded_xh = [sem(f"loaded_xh{i}") for i in range(2)]
        loaded_xt = [sem(f"loaded_xt{i}") for i in range(2)]
        stored = [sem(f"stored{i}") for i in range(2)]
        prep = sem("prep")
        step = sem("step")
        enter_turned = sem("enter_turned")
        enter_copied = sem("enter_copied")
        enter_counted = sem("enter_counted")
        centered = sem("centered")
        variance = sem("variance")
        squared = sem("squared")
        logged = sem("logged")
        rooted = sem("rooted")
        normed = sem("normed")
        ones_set = sem("ones_set")
        projected = sem("projected")
        gates_ready = sem("gates_ready")
        gates_masked = sem("gates_masked")
        products_ready = sem("products_ready")
        contracted = sem("contracted")
        copied = sem("copied")
        squares_ready = sem("squares_ready")
        summed = sem("summed")
        sums_cleared = sem("sums_cleared")
        turned = sem("turned")
        gate_projected = sem("gate_projected")
        out_projected = sem("out_projected")
        turned_back = sem("turned_back")
        scaled = sem("scaled")
        gate_ready = sem("gate_ready")
        tokens_ready = sem("tokens_ready")
        mean_off = sem("mean_off")
        gated_ready = sem("gated_ready")
        x_ready = sem("x_ready")
        stats_taken = sem("stats_taken")
        normalized = sem("normalized")
        tick = sem("tick")

        def advance(*counts):
            for sem_, n in counts:
                sem_.n += n

        K = lambda c, rows=P: kst[0:rows, c:c + P]
        vec = lambda i, rows=P: prm[0:rows, W_VEC + i:W_VEC + i + 1]

        with nc.Block() as block:
            @block.sync
            def _(sp):
                for s in sems:
                    sp.sem_inc(s.s, CREDIT)
                sp.dma_start(kst[:, :], consts).then_inc(prep.s, 16)
                sp.wait_ge(prep.s, prep.n + 16)

            @block.vector
            def _(dve):
                dve.memset(eps1[:, :], EPS)
        advance((prep, 16))

        def pair_chunk(dram, ut, vb):
            return dram[bass.ds(8 * ut, 8), :, bass.ds(vb * 256, 256)].rearrange("g p f -> p g f")

        def xh_chunk(n, k_is_b):
            if k_is_b:
                return XH[bass.ds(n, 1), :, :].rearrange("o p f -> p (o f)")
            return XHA[:, bass.ds(n * COLS, COLS)]

        def pair_cols(buf, q):
            return buf.rearrange("p (g f) -> p g f", g=8)[:, :, 64 * q:64 * q + 64]

        def by_b(buf, q):
            return buf.rearrange("p (j g r) -> p g j r", g=8, r=16)[:, :, 4 * q:4 * q + 4, :]

        ar = Arena()
        e_x = [ar.take(COLS) for _ in range(2)]
        e_t = [ar.take(COLS) for _ in range(2)]
        x_nat = x_in.rearrange("o (t a) (s v) c -> (o t) a s v c", t=NT, s=2)
        with nc.Block() as block:
            @block.sync
            def _(sp):
                with sp.Fori(0, NCH // 2) as i:
                    for h in range(2):
                        n = 2 * i + h
                        sp.wait_ge(enter_turned.s, enter_turned.n + 4 * n - 4)
                        sp.sem_inc(tick.s, 1)
                        ut, vb = i // 4, (2 * i + h) % 8
                        for s in range(2):
                            sp.dma_start(e_x[h].rearrange("p (v s c) -> p s v c", s=2, c=C)[:, s, :, :],
                                         x_nat[ut, :, s, bass.ds(vb * 16, 16), :]) \
                                .then_inc(loaded[h].s, 16)
                sp.wait_ge(stored[0].s, stored[0].n + 8 * NCH)
                sp.wait_ge(stored[1].s, stored[1].n + 8 * NCH)

            @block.tensor
            def _(pe):
                with pe.Fori(0, NCH // 2) as i:
                    for h in range(2):
                        pe.wait_ge(loaded[h].s, loaded[h].n + 32 * i + 32)
                        for q in range(4):
                            b = 4 * h + q
                            pe.wait_ge(enter_copied.s, enter_copied.n + 8 * i + b - 7)
                            for j in range(4):
                                last = pe.transpose(
                                    bank(b).rearrange("p (g j r) -> p g j r", g=8, j=4)[:, :, j, :],
                                    e_x[h][:, (4 * q + j) * P:(4 * q + j + 1) * P], K(K_IDENT))
                            last.then_inc(enter_turned.s, 1)

            @block.scalar
            def _(act):
                with act.Fori(0, NCH // 2) as i:
                    for h in range(2):
                        act.wait_ge(stored[h].s, stored[h].n + 16 * i)
                        act.wait_ge(enter_counted.s, enter_counted.n + 8 * i + 4 * h - 4)
                        for q in range(4):
                            act.wait_ge(enter_turned.s, enter_turned.n + 8 * i + 4 * h + q + 1)
                            act.activation(pair_cols(e_t[h], q),
                                           bank(4 * h + q).rearrange("p (g f) -> p g f", g=8),
                                           ACT.Copy).then_inc(enter_copied.s, 1)
                        act.wait_ge(enter_copied.s, enter_copied.n + 8 * i + 4 * h + 4)
                        ut, vb = i // 4, (2 * i + h) % 8
                        act.dma_start(pair_chunk(XT, ut, vb), e_t[h].rearrange("p (g f) -> p g f", g=8)) \
                            .then_inc(stored[h].s, 16)

            @block.vector
            def _(dve):
                with dve.Fori(0, NCH // 2) as i:
                    for h in range(2):
                        for q in range(4):
                            dve.wait_ge(enter_copied.s, enter_copied.n + 8 * i + 4 * h + q + 1)
                            dve.bn_stats(stats[:, bass.ds(8 * i + 4 * h + q, 1), :]
                                         .rearrange("p o f -> p (o f)"),
                                         pair_cols(e_t[h], q)) \
                                .then_inc(enter_counted.s, 1)
        advance((loaded[0], 16 * NCH), (loaded[1], 16 * NCH), (stored[0], 16 * NCH // 2),
            (stored[1], 16 * NCH // 2), (enter_turned, 4 * NCH), (enter_copied, 4 * NCH), (enter_counted, 4 * NCH))


        def prepare(number, layer):
            mean, var = small[:, 0:1], small[:, 1:2]
            dev, second, std, a, b, cb = (small[:, i:i + 1] for i in range(2, 8))
            w_cat = prm[0:C, W_CAT:W_CAT + 320]
            loads = 2 if layer["masked"] else 1
            with nc.Block() as block:
                @block.sync
                def _(sp):
                    sp.dma_start(prm[:, :], params[number]).then_inc(prep.s, 16)
                    if layer["masked"]:
                        sp.dma_start(mask_sb[:, :, :], masks[number // 2]).then_inc(prep.s, 16)

                @block.tensor
                def _(pe):
                    pe.wait_ge(step.s, step.n + 1)
                    pe.matmul(bank(0)[:, 0:1], K(K_GROUP), mean, start=True, stop=True).then_inc(step.s, 1)
                    pe.wait_ge(step.s, step.n + 5)
                    pe.matmul(bank(1)[:, 0:1], K(K_GROUP), second, start=True, stop=True).then_inc(step.s, 1)
                    pe.wait_ge(step.s, step.n + 11)
                    pe.matmul(bank(2)[:, 0:1], K(K_CENTER), b, start=True, stop=True).then_inc(step.s, 1)
                    pe.wait_ge(step.s, step.n + 15)
                    pe.matmul(bank(3)[:, 0:320], K(K_DROP, C), wfold[:, :], start=True, stop=False)
                    pe.matmul(bank(3)[:, 0:320], bfirst[:, :], w_cat, start=False, stop=False)
                    pe.matmul(bank(3)[:, 0:320], K(K_FIRST, 1), prm[0:1, W_BIAS:W_BIAS + 320],
                              start=False, stop=True).then_inc(step.s, 1)

                @block.scalar
                def _(act):
                    act.wait_ge(step.s, step.n + 6)
                    act.activation(std, bank(1)[:, 0:1], ACT.Sqrt, bias=eps1[:, :]).then_inc(step.s, 1)

                @block.vector
                def _(dve):
                    dve.bn_aggr(small[:, 0:2], stats[:, :, :].rearrange("p t f -> p (t f)")).then_inc(step.s, 1)
                    dve.wait_ge(step.s, step.n + 2)
                    dve.tensor_tensor(dev, mean, bank(0)[:, 0:1], ALU.subtract).then_inc(step.s, 1)
                    dve.wait_ge(step.s, step.n + 3)
                    dve.tensor_tensor(second, dev, dev, ALU.mult).then_inc(step.s, 1)
                    dve.wait_ge(step.s, step.n + 4)
                    dve.tensor_tensor(second, second, var, ALU.add).then_inc(step.s, 1)
                    dve.wait_ge(step.s, step.n + 7)
                    dve.reciprocal(a, std).then_inc(step.s, 1)
                    dve.wait_ge(step.s, step.n + 8)
                    dve.tensor_tensor(b, a, bank(0)[:, 0:1], ALU.mult).then_inc(step.s, 1)
                    dve.wait_ge(step.s, step.n + 9)
                    dve.tensor_scalar(cen[:, :], K(K_CENTER), a, None, ALU.mult).then_inc(step.s, 1)
                    dve.wait_ge(step.s, step.n + 10)
                    dve.tensor_scalar(b, b, -1.0, None, ALU.mult).then_inc(step.s, 1)
                    dve.wait_ge(step.s, step.n + 12)
                    dve.tensor_copy(cb, bank(2)[:, 0:1]).then_inc(step.s, 1)
                    dve.wait_ge(prep.s, prep.n + 16 * loads)
                    dve.tensor_scalar(wfold[:, :], w_cat, vec(V_NW, C), None, ALU.mult).then_inc(step.s, 1)
                    dve.tensor_scalar(bfirst[:, :], K(K_FIRST, C), vec(V_NB, C), None, ALU.mult).then_inc(step.s, 1)
                    dve.memset(wog[:, :], 0.0).then_inc(step.s, 1)
                    dve.wait_ge(step.s, step.n + 17)
                    dve.tensor_copy(wproj[:, :], bank(3)[:, 0:320]).then_inc(step.s, 1)
                    for s in range(2):
                        dve.tensor_copy(wog[C * s:C * s + C, C * s:C * s + C],
                                        bank(3)[C * s:C * s + C, 256:320]).then_inc(step.s, 1)
            advance((prep, 16 * loads), (step, 20))

        def norm(number, layer):
            ar = Arena()
            xa = [ar.take(COLS) for _ in range(2)]
            xo = [ar.take(COLS) for _ in range(2)]
            sq = [ar.take(GW) for _ in range(2)]
            lnv = [ar.take(GW) for _ in range(2)]
            rs = [ar.take(GW) for _ in range(2)]
            cb, k_is_b = small[:, 7:8], layer["k_is_b"]
            cut = lambda t: slice(t * GW, (t + 1) * GW)
            with nc.Block() as block:
                @block.sync
                def _(sp):
                    def load(n, h):
                        if k_is_b:
                            sp.dma_start(xa[h], XT[bass.ds(n, 1), :, :].rearrange("o p f -> p (o f)")) \
                                .then_inc(loaded[h].s, 16)
                        else:
                            sp.dma_start(xa[h].rearrange("p (g f) -> p g f", g=16),
                                         XT[:, :, bass.ds(n * 128, 128)].rearrange("g p f -> p g f")) \
                                .then_inc(loaded[h].s, 16)

                    def store(n, h):
                        sp.wait_ge(ones_set.s, ones_set.n + 2 * n + 2)
                        sp.sem_inc(tick.s, 1)
                        sp.dma_start(xh_chunk(n, k_is_b), xo[h]).then_inc(stored[h].s, 16)

                    for h in range(2):
                        load(h, h)
                    with sp.Fori(0, NCH // 2 - 1) as i:
                        for h in range(2):
                            sp.wait_ge(centered.s, centered.n + 4 * i + 2 * h + 2)
                            sp.sem_inc(tick.s, 1)
                            load(2 * i + h + 2, h)
                            store(2 * i + h, h)
                    for h in range(2):
                        store(NCH - 2 + h, h)
                    for h in range(2):
                        sp.wait_ge(stored[h].s, stored[h].n + 8 * NCH)

                @block.tensor
                def _(pe):
                    with pe.Fori(0, NCH // 2) as i:
                        for h in range(2):
                            pe.wait_ge(loaded[h].s, loaded[h].n + 16 * i + 16)
                            for t in range(2):
                                tile = 4 * i + 2 * h + t
                                pe.wait_ge(normed.s, normed.n + tile - 1)
                                for u in range(2):
                                    at = 2 * t + u
                                    cols = xa[h][:, at * BANK:(at + 1) * BANK] if k_is_b else \
                                        xa[h].rearrange("p (g j r) -> p j g r", g=16, j=8)[:, 2 * at:2 * at + 2, :, :]
                                    last = pe.matmul(banks[t][:, u * BANK:(u + 1) * BANK], cen[:, :], cols,
                                                     start=True, stop=True)
                                last.then_inc(centered.s, 1)
                            for t in range(2):
                                tile = 4 * i + 2 * h + t
                                pe.wait_ge(squared.s, squared.n + tile + 1)
                                pe.wait_ge(logged.s, logged.n + tile - 1)
                                for u in range(2):
                                    last = pe.matmul(banks[2 + t][:, u * BANK:(u + 1) * BANK], K(K_MEAN),
                                                     sq[t][:, u * BANK:(u + 1) * BANK], start=True, stop=True)
                                last.then_inc(variance.s, 1)

                @block.scalar
                def _(act):
                    with act.Fori(0, NCH // 2) as i:
                        for h in range(2):
                            for t in range(2):
                                tile = 4 * i + 2 * h + t
                                act.wait_ge(centered.s, centered.n + tile + 1)
                                act.wait_ge(variance.s, variance.n + tile - 1)
                                act.activation(sq[t], banks[t][:, :], ACT.Square, bias=cb).then_inc(squared.s, 1)
                            for t in range(2):
                                tile = 4 * i + 2 * h + t
                                act.wait_ge(variance.s, variance.n + tile + 1)
                                act.wait_ge(rooted.s, rooted.n + tile - 1)
                                act.activation(lnv[t], banks[2 + t][:, :], ACT.Ln, bias=eps1[:, :]) \
                                    .then_inc(logged.s, 1)
                                act.wait_ge(logged.s, logged.n + tile + 1)
                                act.wait_ge(normed.s, normed.n + tile - 1)
                                act.activation(rs[t], lnv[t], ACT.Exp, scale=-0.5).then_inc(rooted.s, 1)

                @block.vector
                def _(dve):
                    with dve.Fori(0, NCH // 2) as i:
                        for h in range(2):
                            dve.wait_ge(stored[h].s, stored[h].n + 16 * i)
                            for t in range(2):
                                dve.wait_ge(rooted.s, rooted.n + 4 * i + 2 * h + t + 1)
                                dve.scalar_tensor_tensor(xo[h][:, cut(t)], banks[t][:, :], cb, rs[t],
                                                         ALU.add, ALU.mult).then_inc(normed.s, 1)

                @block.gpsimd
                def _(pool):
                    with pool.Fori(0, NCH // 2) as i:
                        for h in range(2):
                            pool.wait_ge(normed.s, normed.n + 4 * i + 2 * h + 2)
                            pool.sem_inc(tick.s, 1)
                            for s in range(2):
                                pool.memset(xo[h][C * s:C * s + 1, :], 1.0).then_inc(ones_set.s, 1)
            advance((loaded[0], 16 * NCH // 2), (loaded[1], 16 * NCH // 2), (stored[0], 16 * NCH // 2),
                (stored[1], 16 * NCH // 2), (centered, 2 * NCH), (variance, 2 * NCH), (squared, 2 * NCH),
                (logged, 2 * NCH), (rooted, 2 * NCH), (normed, 2 * NCH), (ones_set, 2 * NCH))

        def project(number, layer, half):
            k_is_b, masked = layer["k_is_b"], layer["masked"]
            dest = LRb if layer["low"] else LR
            w = [wproj[C * s:C * s + C, half * P:(half + 1) * P] for s in range(2)]
            gate = msg if masked else sig
            used, gates = (gates_masked, gates_masked) if masked else (products_ready, gates_ready)

            def where(n, g):
                if k_is_b:
                    return g // 2, g // 2, 16 * n + 8 * (g % 2)
                return g // 2, g % 2, P * (g // 2) + 8 * n

            with nc.Block() as block:
                @block.sync
                def _(sp):
                    with sp.Fori(0, NCH // 2) as i:
                        for h in range(2):
                            n = 2 * i + h
                            sp.wait_ge(projected.s, projected.n + 4 * n - 4)
                            sp.sem_inc(tick.s, 1)
                            sp.dma_start(xh_b[h], xh_chunk(n, k_is_b)).then_inc(loaded[h].s, 16)

                @block.tensor
                def _(pe):
                    with pe.Fori(0, NCH // 2) as i:
                        for h in range(2):
                            pe.wait_ge(loaded[h].s, loaded[h].n + 16 * i + 16)
                            for g in range(4):
                                s, kt, _ = where(0, g)
                                rows = slice(C * s, C * s + C)
                                pe.wait_ge(products_ready.s, products_ready.n + 8 * i + 4 * h + g - 3)
                                for j in range(8):
                                    if k_is_b:
                                        tokens = xh_b[h][rows, :].rearrange("p (b r) -> p b r", r=16)[:, :, 8 * (g % 2) + j]
                                    else:
                                        tokens = xh_b[h][rows, j * N + kt * P:j * N + (kt + 1) * P]
                                    last = pe.matmul(banks[g][:, j * P:(j + 1) * P], tokens, w[s], start=True, stop=True)
                                last.then_inc(projected.s, 1)

                @block.scalar
                def _(act):
                    with act.Fori(0, NCH // 2) as i:
                        for h in range(2):
                            for g in range(4):
                                group = 8 * i + 4 * h + g
                                act.wait_ge(projected.s, projected.n + group + 1)
                                act.wait_ge(used.s, used.n + group - 1)
                                act.activation(sig[g % 2][:, :, :],
                                               banks[g][:, :].rearrange("p (m c) -> p c m", m=8)[:, C:, :],
                                               ACT.Sigmoid).then_inc(gates_ready.s, 1)

                if masked:
                    @block.gpsimd
                    def _(pool):
                        with pool.Fori(0, NCH // 2) as i:
                            for h in range(2):
                                for g in range(4):
                                    group = 8 * i + 4 * h + g
                                    _, kt, m = where(2 * i + h, g)
                                    pool.wait_ge(gates_ready.s, gates_ready.n + group + 1)
                                    pool.wait_ge(products_ready.s, products_ready.n + group - 1)
                                    pool.tensor_tensor(msg[g % 2][:, :, :], sig[g % 2][:, :, :],
                                                       mask_sb[:, kt, bass.ds(m, 8)].unsqueeze(1).broadcast_to([P, C, 8]),
                                                       ALU.mult).then_inc(gates_masked.s, 1)

                @block.vector
                def _(dve):
                    with dve.Fori(0, NCH // 2) as i:
                        for h in range(2):
                            for g in range(4):
                                _, kt, m = where(2 * i + h, g)
                                dve.wait_ge(gates.s, gates.n + 8 * i + 4 * h + g + 1)
                                dve.tensor_tensor(dest[:, kt, :, bass.ds(m, 8)],
                                                  banks[g][:, :].rearrange("p (m c) -> p c m", m=8)[:, 0:C, :],
                                                  gate[g % 2][:, :, :], ALU.mult).then_inc(products_ready.s, 1)
            advance((loaded[0], 16 * NCH // 2), (loaded[1], 16 * NCH // 2), (projected, 4 * NCH),
                (gates_ready, 4 * NCH), (products_ready, 4 * NCH))
            if masked:
                advance((gates_masked, 4 * NCH))

        def contract(number, layer, half):
            low = layer["low"]
            src = LRb if low else LR
            off_a, off_b = (0, HALF) if layer["left_a"] else (HALF, 0)
            hold = [(o[:, :].bitcast(BF16)[:, 0:16 * 256] if low else o[:, :]) for o in obuf]
            by_block = [o.rearrange("p (v c r) -> p v c r", v=16, c=16) for o in hold]
            by_channel = [o.rearrange("p (v c r) -> p c v r", v=16, c=16) for o in hold]
            parts = [(piece, g) for piece in range(4) for g in range(4)]
            with nc.Block() as block:
                @block.tensor
                def _(pe):
                    for e, (piece, g) in enumerate(parts):
                        cq, ut = divmod(piece, 2)
                        if e >= 4:
                            pe.wait_ge(copied.s, copied.n + e - 3)
                        for c in range(4):
                            ch = 16 * cq + 4 * g + c
                            for kt in range(NT):
                                last = pe.matmul(banks[e % 4][:, c * N:(c + 1) * N],
                                                 src[:, kt, off_a + ch, ut * P:(ut + 1) * P],
                                                 src[:, kt, off_b + ch, :], start=kt == 0, stop=kt == NT - 1)
                        last.then_inc(contracted.s, 1)

                @block.scalar
                def _(act):
                    for e, (piece, g) in enumerate(parts):
                        if piece >= 2 and g == 0:
                            act.wait_ge(stored[piece % 2].s, stored[piece % 2].n + 16)
                            act.wait_ge(summed.s, summed.n + 4 * 4 * (piece - 1))
                        act.wait_ge(contracted.s, contracted.n + e + 1)
                        act.activation(by_channel[piece % 2][:, 4 * g:4 * g + 4, :, :],
                                       banks[e % 4][:, :].rearrange("p (c v r) -> p c v r", c=4, r=16),
                                       ACT.Copy).then_inc(copied.s, 1)
                        act.wait_ge(copied.s, copied.n + e + 1)
                        if e >= 2:
                            act.wait_ge(summed.s, summed.n + 4 * (e - 1))
                        act.activation(squares[e % 2][:, :].rearrange("p (c v r) -> p c v r", c=4, r=16),
                                       by_channel[piece % 2][:, 4 * g:4 * g + 4, :, :],
                                       ACT.Square).then_inc(squares_ready.s, 1)

                @block.vector
                def _(dve):
                    if half == 0:
                        dve.memset(sum1[:, :, :], 0.0).then_inc(sums_cleared.s, 1)
                        dve.memset(sum2[:, :, :], 0.0).then_inc(sums_cleared.s, 1)
                        dve.wait_ge(sums_cleared.s, sums_cleared.n + 2)
                    for e, (piece, g) in enumerate(parts):
                        ut = piece % 2
                        for two in range(2):
                            if two == 0:
                                dve.wait_ge(copied.s, copied.n + e + 1)
                            if e or two:
                                dve.wait_ge(summed.s, summed.n + 4 * e + 2 * two - 1)
                            dve.tensor_tensor(sum1[:, ut, :].rearrange("p (c v r) -> p c v r", c=2, r=16),
                                              sum1[:, ut, :].rearrange("p (c v r) -> p c v r", c=2, r=16),
                                              by_channel[piece % 2][:, 4 * g + 2 * two:4 * g + 2 * two + 2, :, :],
                                              ALU.add).then_inc(summed.s, 1)
                            if two == 0:
                                dve.wait_ge(squares_ready.s, squares_ready.n + e + 1)
                            if e or two:
                                dve.wait_ge(summed.s, summed.n + 4 * e + 2 * two)
                            dve.tensor_tensor(sum2[:, ut, :], sum2[:, ut, :],
                                              squares[e % 2][:, 2 * two * N:2 * (two + 1) * N],
                                              ALU.add).then_inc(summed.s, 1)

                @block.sync
                def _(sp):
                    for piece in range(4):
                        cq, ut = divmod(piece, 2)
                        sp.wait_ge(copied.s, copied.n + 4 * (piece + 1))
                        sp.dma_start((OSL if low else OS)[ut, :, 2 * half + cq, :, :].rearrange("v p f -> p v f"),
                                     hold[piece % 2].rearrange("p (v f) -> p v f", v=16)) \
                            .then_inc(stored[piece % 2].s, 16)
                    for h in range(2):
                        sp.wait_ge(stored[h].s, stored[h].n + 32)
            advance((contracted, 16), (copied, 16), (squares_ready, 16), (summed, 64), (stored[0], 32), (stored[1], 32))
            if half == 0:
                advance((sums_cleared, 2))

        def moments(number, layer):
            s1 = [sum1[:, :, i * N:(i + 1) * N] for i in range(2)]
            s2 = [sum2[:, :, i * N:(i + 1) * N] for i in range(2)]
            with nc.Block() as block:
                @block.vector
                def _(dve):
                    at = [0]

                    def then(ins):
                        at[0] += 1
                        ins.then_inc(step.s, 1)
                        dve.wait_ge(step.s, step.n + at[0])

                    then(dve.memset(epso[:, :], EPS * layer["div"] ** 2))
                    then(dve.tensor_tensor(s1[0], s1[0], s1[1], ALU.add))
                    then(dve.tensor_scalar(s1[0], s1[0], 1.0 / C, None, ALU.mult))
                    then(dve.tensor_tensor(s2[0], s2[0], s2[1], ALU.add))
                    then(dve.tensor_tensor(s1[1], s1[0], s1[0], ALU.mult))
                    then(dve.scalar_tensor_tensor(s2[0], s2[0], 1.0 / C, s1[1], ALU.mult, ALU.subtract))
                    dve.tensor_scalar(s2[0], s2[0], 0.0, None, ALU.max).then_inc(step.s, 1)
                    dve.wait_ge(step.s, step.n + 8)
                    dve.reciprocal(s2[0], s2[1]).then_inc(step.s, 1)

                @block.scalar
                def _(act):
                    act.wait_ge(step.s, step.n + 7)
                    act.activation(s2[1], s2[0], ACT.Sqrt, bias=epso[:, :]).then_inc(step.s, 1)
            advance((step, 9))

        def finish(number, layer):
            low, gate_first, end = layer["low"], layer["gate_first"], number == len(LAYERS) - 1
            k_is_b = layer["k_is_b"]
            ar = Arena()
            o_in = [ar.take(COLS) for _ in range(2)]
            nrm = [ar.take(COLS) for _ in range(2)]
            xh = [ar.take(COLS) for _ in range(2)]
            xi = [ar.take(COLS) for _ in range(2)]
            xo = [ar.take(COLS) for _ in range(2)]
            nat = [ar.take(COLS) for _ in range(2)]
            aff = [ar.take(BANK) for _ in range(2)]
            og = [ar.take(BANK) for _ in range(2)]
            gated = [ar.take(BANK) for _ in range(2)]
            o_v = [(o.bitcast(BF16)[:, 0:COLS] if low else o).rearrange("p (s c v) -> p s c v", s=2, c=C) for o in o_in]
            n_v = [o.rearrange("p (v s c) -> p s c v", s=2, c=C) for o in nrm]
            w_out = prm[:, W_OUT:W_OUT + P]
            out_nat = out.rearrange("o (t a) (s v) c -> t (o a) s (v c)", t=NT, s=2)
            fed, taken, aff_used = (gated_ready, x_ready, gated_ready) if gate_first else (scaled, gated_ready, out_projected)

            def at(n_half, h):
                return n_half // 4, (2 * n_half + h) % 8

            def token(t, i, h):
                ut, vb = at(i, h)
                v = t[:, bass.ds(ut, 1), 0:N].rearrange("p o (s v) -> p (o s) v", s=2)[:, :, bass.ds(16 * vb, 16)]
                return v.unsqueeze(2).broadcast_to([P, 2, C, 16])

            with nc.Block() as block:
                @block.sync
                def _(sp):
                    def load(i, h, first):
                        ut, vb = at(i, h)
                        if not first:
                            sp.wait_ge(mean_off.s, mean_off.n + 2 * i + h - 1)
                            sp.sem_inc(tick.s, 1)
                            sp.wait_ge(gate_projected.s, gate_projected.n + 8 * i + 4 * h - 4)
                            sp.sem_inc(tick.s, 1)
                            sp.wait_ge(x_ready.s, x_ready.n + 8 * i + 4 * h - 4)
                            sp.sem_inc(tick.s, 1)
                        o = o_in[h].bitcast(BF16)[:, 0:COLS] if low else o_in[h]
                        for s in range(2):
                            sp.dma_start(o[:, s * 1024:(s + 1) * 1024].rearrange("p (q f) -> p q f", q=4),
                                         (OSL if low else OS)[ut, 8 * s + vb if first else bass.ds(8 * s + vb, 1)]
                                         .rearrange("q p f -> p q f" if first else "o q p f -> p (o q) f")) \
                                .then_inc(loaded[h].s, 16)
                        if k_is_b:
                            sp.dma_start(xh[h].rearrange("p (g f) -> p g f", g=8), pair_chunk(XH, ut, vb)) \
                                .then_inc(loaded_xh[h].s, 16)
                        else:
                            sp.dma_start(xh[h].rearrange("p (j a) -> p j a", j=16),
                                         XHA.rearrange("p (b a) -> p b a", a=N)[
                                             :, bass.ds(16 * vb, 16), bass.ds(P * ut, P)]) \
                                .then_inc(loaded_xh[h].s, 16)
                        sp.dma_start(xi[h].rearrange("p (g f) -> p g f", g=8), pair_chunk(XT, ut, vb)) \
                            .then_inc(loaded_xt[h].s, 16)

                    def store(i, h):
                        ut, vb = at(i, h)
                        if end:
                            sp.wait_ge(tokens_ready.s, tokens_ready.n + 8 * i + 4 * h + 4)
                            sp.sem_inc(tick.s, 1)
                            sp.dma_start(out_nat[ut, :, :, bass.ds(vb * 1024, 1024)],
                                         nat[h].rearrange("p (s f) -> p s f", s=2)).then_inc(stored[h].s, 16)
                        else:
                            sp.wait_ge(x_ready.s, x_ready.n + 8 * i + 4 * h + 4)
                            sp.sem_inc(tick.s, 1)
                            sp.dma_start(pair_chunk(XT, ut, vb), xo[h].rearrange("p (g f) -> p g f", g=8)) \
                                .then_inc(stored[h].s, 16)

                    for h in range(2):
                        load(0, h, True)
                    with sp.Fori(0, NCH // 2 - 1) as i:
                        for h in range(2):
                            load(i + 1, h, False)
                            store(i, h)
                    for h in range(2):
                        store(NCH // 2 - 1, h)
                    for h in range(2):
                        sp.wait_ge(stored[h].s, stored[h].n + 8 * NCH)

                @block.tensor
                def _(pe):
                    with pe.Fori(0, NCH // 2) as i:
                        for h in range(2):
                            def turn(q):
                                tile = 8 * i + 4 * h + q
                                pe.wait_ge(scaled.s, scaled.n + tile - 1)
                                for j in range(4):
                                    last = pe.transpose(
                                        bank(q % 2).rearrange("p (g j r) -> p g j r", g=8, j=4)[:, :, j, :],
                                        nrm[h][:, (4 * q + j) * P:(4 * q + j + 1) * P], K(K_IDENT))
                                last.then_inc(turned.s, 1)

                            def out_gate(q):
                                pe.wait_ge(gate_ready.s, gate_ready.n + 8 * i + 4 * h + q - 1)
                                pe.matmul(bank(2 + q % 2), wog[:, :],
                                          pair_cols(xh[h], q) if k_is_b else by_b(xh[h], q),
                                          start=True, stop=True).then_inc(gate_projected.s, 1)

                            def project_out(q):
                                tile = 8 * i + 4 * h + q
                                pe.wait_ge(fed.s, fed.n + tile + 1)
                                pe.wait_ge(taken.s, taken.n + tile - 1)
                                pe.matmul(bank(4 + q % 2), w_out, (gated if gate_first else aff)[q % 2],
                                          start=True, stop=True).then_inc(out_projected.s, 1)

                            def turn_back(q):
                                tile = 8 * i + 4 * h + q
                                pe.wait_ge(x_ready.s, x_ready.n + tile + 1)
                                pe.wait_ge(tokens_ready.s, tokens_ready.n + tile - 1)
                                for j in range(4):
                                    last = pe.transpose(bank(6 + q % 2)[:, j * P:(j + 1) * P],
                                                        xo[h][:, (4 * q + j) * P:(4 * q + j + 1) * P], K(K_IDENT))
                                last.then_inc(turned_back.s, 1)

                            pe.wait_ge(normalized.s, normalized.n + 2 * i + h + 1)
                            pe.wait_ge(loaded_xh[h].s, loaded_xh[h].n + 16 * i + 16)
                            for q in range(4):
                                turn(q)
                                out_gate(q)
                                if q:
                                    project_out(q - 1)
                                if end and q > 1:
                                    turn_back(q - 2)
                            project_out(3)
                            if end:
                                turn_back(2)
                                turn_back(3)

                @block.scalar
                def _(act):
                    with act.Fori(0, NCH // 2) as i:
                        for h in range(2):
                            def back(q):
                                if q == 0:
                                    act.wait_ge(stored[h].s, stored[h].n + 16 * i)
                                act.wait_ge(turned_back.s, turned_back.n + 8 * i + 4 * h + q + 1)
                                act.activation(
                                    nat[h].rearrange("p (s v c) -> p v s c", s=2, c=C)[:, 4 * q:4 * q + 4, :, :],
                                    bank(6 + q % 2).rearrange("p (j s c) -> p j s c", j=4, s=2),
                                    ACT.Copy).then_inc(tokens_ready.s, 1)

                            for q in range(4):
                                tile = 8 * i + 4 * h + q
                                act.wait_ge(turned.s, turned.n + tile + 1)
                                act.wait_ge(aff_used.s, aff_used.n + tile - 1)
                                act.activation(aff[q % 2], bank(q % 2), ACT.Identity, bias=vec(V_OB),
                                               scale=vec(V_OW)).then_inc(scaled.s, 1)
                                act.wait_ge(gate_projected.s, gate_projected.n + tile + 1)
                                act.wait_ge(gated_ready.s, gated_ready.n + tile - 1)
                                act.activation(og[q % 2], bank(2 + q % 2), ACT.Sigmoid).then_inc(gate_ready.s, 1)
                                if end and q > 1:
                                    back(q - 2)
                            if end:
                                back(2)
                                back(3)

                @block.gpsimd
                def _(pool):
                    with pool.Fori(0, NCH // 2) as i:
                        for h in range(2):
                            pool.wait_ge(mean_off.s, mean_off.n + 2 * i + h + 1)
                            pool.tensor_tensor(n_v[h], n_v[h], token(sum2, i, h), ALU.mult).then_inc(normalized.s, 1)

                @block.vector
                def _(dve):
                    def center(i, h):
                        dve.wait_ge(loaded[h].s, loaded[h].n + 32 * i + 32)
                        dve.wait_ge(turned.s, turned.n + 8 * i + 4 * h - 4)
                        dve.tensor_tensor(n_v[h], o_v[h], token(sum1, i, h), ALU.subtract).then_inc(mean_off.s, 1)

                    with dve.Fori(0, NCH // 2) as i:
                        for h in range(2):
                            def gate(q):
                                tile = 8 * i + 4 * h + q
                                dve.wait_ge(scaled.s, scaled.n + tile + 1)
                                dve.wait_ge(gate_ready.s, gate_ready.n + tile + 1)
                                dve.wait_ge(out_projected.s, out_projected.n + tile - 1)
                                dve.tensor_tensor(gated[q % 2], aff[q % 2], og[q % 2], ALU.mult) \
                                    .then_inc(gated_ready.s, 1)

                            def add(q):
                                tile = 8 * i + 4 * h + q
                                if q == 0:
                                    dve.wait_ge(loaded_xt[h].s, loaded_xt[h].n + 16 * i + 16)
                                    dve.wait_ge(stored[h].s, stored[h].n + 16 * i)
                                dve.wait_ge(out_projected.s, out_projected.n + tile + 1)
                                tall = lambda v: v.rearrange("p (g f) -> p g f", g=8)
                                if gate_first:
                                    dve.scalar_tensor_tensor(pair_cols(xo[h], q), tall(bank(4 + q % 2)), vec(V_BO),
                                                             pair_cols(xi[h], q), ALU.add, ALU.add) \
                                        .then_inc(x_ready.s, 1)
                                else:
                                    dve.wait_ge(gate_ready.s, gate_ready.n + tile + 1)
                                    dve.wait_ge(x_ready.s, x_ready.n + tile - 1)
                                    dve.scalar_tensor_tensor(gated[q % 2], bank(4 + q % 2), vec(V_BO), og[q % 2],
                                                             ALU.add, ALU.mult).then_inc(gated_ready.s, 1)
                                    dve.wait_ge(gated_ready.s, gated_ready.n + tile + 1)
                                    cols = lambda v: pair_cols(v, q).rearrange("p g (j r) -> p g j r", r=16)
                                    dve.tensor_tensor(by_b(xo[h], q) if end else cols(xo[h]),
                                                      gated[q % 2].rearrange("p (g j r) -> p g j r", g=8, j=4),
                                                      cols(xi[h]), ALU.add).then_inc(x_ready.s, 1)
                                if not end:
                                    dve.wait_ge(x_ready.s, x_ready.n + tile + 1)
                                    dve.bn_stats(stats[:, bass.ds(tile, 1), :].rearrange("p o f -> p (o f)"),
                                                 pair_cols(xo[h], q)).then_inc(stats_taken.s, 1)

                            center(i, h)
                            if gate_first:
                                for q in range(4):
                                    gate(q)
                                    if q:
                                        add(q - 1)
                                add(3)
                            else:
                                for q in range(4):
                                    add(q)
            advance((loaded[0], 16 * NCH), (loaded[1], 16 * NCH), (loaded_xh[0], 16 * NCH // 2),
                (loaded_xh[1], 16 * NCH // 2), (loaded_xt[0], 16 * NCH // 2), (loaded_xt[1], 16 * NCH // 2),
                (stored[0], 16 * NCH // 2), (stored[1], 16 * NCH // 2), (turned, 4 * NCH),
                (gate_projected, 4 * NCH), (out_projected, 4 * NCH), (scaled, 4 * NCH), (gate_ready, 4 * NCH),
                (mean_off, NCH), (gated_ready, 4 * NCH), (x_ready, 4 * NCH), (normalized, NCH))
            if end:
                advance((turned_back, 4 * NCH), (tokens_ready, 4 * NCH))
            else:
                advance((stats_taken, 4 * NCH))

        for number, layer in enumerate(LAYERS):
            prepare(number, layer)
            norm(number, layer)
            for half in range(2):
                project(number, layer, half)
                contract(number, layer, half)
            moments(number, layer)
            finish(number, layer)


def constants():
    import numpy as np

    k = np.zeros((P, K_END), np.float32)
    same_half = np.arange(P)[:, None] // C == np.arange(P)[None, :] // C
    channel = np.arange(P) % C
    k[:, K_CENTER:K_CENTER + P] = np.eye(P) - same_half / C
    k[:, K_MEAN:K_MEAN + P] = same_half / C
    k[:, K_GROUP:K_GROUP + P] = (channel[:, None] // 2 == channel[None, :] // 2) / 4
    k[:, K_IDENT:K_IDENT + P] = np.eye(P)
    drop = (channel[:C, None] == channel[None, :]).astype(np.float32)
    drop[0, :] = -1
    drop[:, channel == 0] = 0
    k[:C, K_DROP:K_DROP + P] = drop
    k[:, K_FIRST:K_FIRST + P] = channel[None, :] == 0
    return k


def pack(wl, wr, wlg, wrg, wog, wo, biases, nw, nb, ow, ob, bo):
    import numpy as np

    p = np.zeros((P, W_END), np.float32)
    order = [(m, h) for h in range(2) for m in range(4)]
    mats, vecs = [wl, wr, wlg, wrg], biases[:4]
    for i, (m, h) in enumerate(order):
        p[:C, W_CAT + 32 * i:W_CAT + 32 * i + 32] = mats[m][:, HALF * h:HALF * h + HALF]
        if vecs[m] is not None:
            p[0, W_BIAS + 32 * i:W_BIAS + 32 * i + 32] = vecs[m][HALF * h:HALF * h + HALF]
    p[:C, W_CAT + 256:W_CAT + 320] = wog
    if biases[4] is not None:
        p[0, W_BIAS + 256:W_BIAS + 320] = biases[4]
    for s in range(2):
        p[C * s:C * s + C, W_OUT + C * s:W_OUT + C * s + C] = wo
        for i, v in enumerate((nw, nb, ow, ob, bo)):
            if v is not None:
                p[C * s:C * s + C, W_VEC + i] = v
    return p


def kernel(**inputs):
    import numpy as np
    import concourse.bacc as bacc
    from concourse.bass_utils import run_bass_kernel_spmd as run

    a = {k: np.asarray(v) for k, v in inputs.items()}
    l0 = {k[8:]: v for k, v in a.items() if k.startswith("L0_conv_")}
    l1 = {k[8:]: v for k, v in a.items() if k.startswith("L1_conv_")}
    l2 = {k[8:]: v for k, v in a.items() if k.startswith("L2_conv_")}
    l3 = {k[8:]: v for k, v in a.items() if k.startswith("L3_conv_")}
    params = np.stack([
        pack(l0["w_left"].T, l0["w_right"].T, l0["w_lgate"].T, l0["w_rgate"].T, l0["w_ogate"].T, l0["w_out"].T,
             [None] * 5, l0["norm_w"], l0["norm_b"], l0["onorm_w"], l0["onorm_b"], None),
        pack(l1["Wl"], l1["Wr"], l1["Wlg"], l1["Wrg"], l1["Wog"], l1["Wo"],
             [l1["bl"], l1["br"], l1["blg"], l1["brg"], l1["bog"]],
             l1["norm_a"], l1["norm_b"], l1["on_a"], l1["on_b"], l1["bo"]),
        pack(l2["w_a_p"], l2["w_b_p"], l2["w_a_g"], l2["w_b_g"], l2["w_g"], l2["w_z"],
             [l2["b_a_p"], l2["b_b_p"], l2["b_a_g"], l2["b_b_g"], l2["b_g"]],
             l2["ln_in_scale"], l2["ln_in_bias"], l2["ln_out_scale"], l2["ln_out_bias"], l2["b_z"]),
        pack(l3["Wl"], l3["Wr"], l3["Wlg"], l3["Wrg"], l3["Wog"], l3["Wo"],
             [l3["bl"], l3["br"], l3["blg"], l3["brg"], l3["bog"]],
             l3["ln_in_g"], l3["ln_in_b"], l3["ln_out_g"], l3["ln_out_b"], l3["bo"]),
    ])
    masks = np.stack([np.ascontiguousarray(m[0].T.reshape(NT, P, N).transpose(1, 0, 2))
                      for m in (l0["mask"], l2["mask"])])
    arrays = {"x": np.ascontiguousarray(a["x"]), "masks": masks, "consts": constants(), "params": params}
    nc = bacc.Bacc("TRN2", target_bir_lowering=False, num_devices=1)
    aps = [nc.dram_tensor(name, v.shape, F32, kind="ExternalInput").ap() for name, v in arrays.items()]
    out = nc.dram_tensor("out", a["x"].shape, F32, kind="ExternalOutput").ap()
    build(nc, *aps, out)
    return run(nc, [arrays], core_ids=[0]).results[0]["out"]
```

```python
from contextlib import ExitStack

import concourse.bass as bass
from concourse import mybir

F32 = mybir.dt.float32
BF16 = mybir.dt.bfloat16
F16 = mybir.dt.float16
ALU = mybir.AluOpType
ACT = mybir.ActivationFunctionType

P = 128
N = 256
C = 64
HALF = 32
NT = N // P
BLK = 16
COLS = 2048
NCH = N * N // 2 // COLS
BANK = 512
EPS = 1e-5
GW = 2 * BANK
X_SCALE = 1024.0
W_SCALE = 1024.0
CREDIT = 64

LAYERS = [
    dict(k_is_b=True, masked=True, low=True, left_a=True, gate_first=True, div=1.0),
    dict(k_is_b=False, masked=False, low=False, left_a=False, gate_first=True, div=float(N)),
    dict(k_is_b=True, masked=True, low=False, left_a=True, gate_first=False, div=1.0),
    dict(k_is_b=False, masked=False, low=False, left_a=True, gate_first=False, div=1.0),
]

K_CENTER, K_MEAN, K_GROUP, K_IDENT, K_DROP, K_FIRST, K_KEEP, K_ONE, K_END = 0, 128, 256, 384, 512, 640, 768, 769, 770
W_CAT, W_BIAS, W_OUT, W_VEC, W_END = 0, 320, 640, 768, 773
V_NW, V_NB, V_OW, V_OB, V_BO = range(5)


class Sem:

    def __init__(self, handle):
        self.s, self.n = handle, CREDIT

    def past(self, n):
        return self.base + n


def pipeline(eng, rounds, per, *stages):
    for k in range(per):
        for run, lag in stages:
            if k >= lag:
                run(0, k - lag)
    with eng.Fori(1, rounds) as i:
        for k in range(per):
            for run, lag in stages:
                run(i if k >= lag else i - 1, (k - lag) % per)
    for k in range(max(lag for _, lag in stages)):
        for run, lag in stages:
            if k < lag:
                run(rounds - 1, per + k - lag)


def build(nc, x_in, masks, consts, params, out):
    ctx = ExitStack()
    with ctx:
        def sb(name, shape, dt=F32):
            return ctx.enter_context(nc.sbuf_tensor(name, shape, dt))

        sems = []

        def sem(name):
            s = Sem(ctx.enter_context(nc.semaphore(name)))
            sems.append(s)
            return s

        XT = nc.dram_tensor("XT", [NCH, P, COLS], F32).ap()
        XH = nc.dram_tensor("XH", [NCH, 2, P, COLS], F16).ap()
        XHA = nc.dram_tensor("XHA", [2, P, NT, N // 2, P], F16).ap()
        OS = nc.dram_tensor("OS", [NT, N // 16, 4, P, 256], F32).ap()
        OSL = nc.dram_tensor("OSL", [NT, N // 16, 4, P, 256], BF16).ap()

        LR = sb("LR", [P, NT, C, N])
        LRb = LR[:, :, :, :].rearrange("p t c m -> p (t c m)").bitcast(BF16)[:, 0:NT * C * N] \
            .rearrange("p (t c m) -> p t c m", t=NT, c=C)
        flat = LR[:, :, :, :].rearrange("p t c m -> p (t c m)")

        class Arena:

            def __init__(self):
                self.at = 0

            def take(self, cols):
                v = flat[:, self.at:self.at + cols]
                self.at += cols
                assert self.at <= NT * C * N
                return v

        obuf = [sb(f"obuf{i}", [P, 16 * 256]) for i in range(2)]
        xh_b = [[o[:, s * COLS // 2:(s + 1) * COLS // 2].bitcast(F16) for s in range(2)] for o in obuf]
        sig = [sb(f"sig{i}", [P, C, 8]) for i in range(2)]
        msg = [sb(f"msg{i}", [P, C, 8]) for i in range(2)]
        squares = [sb(f"squares{i}", [P, 4 * N]) for i in range(2)]
        sum1 = sb("sum1", [P, NT, 2 * N])
        sum2 = sb("sum2", [P, NT, 2 * N])
        mask_sb = sb("mask_sb", [P, NT, N])
        kst = sb("kst", [P, K_END])
        prm = sb("prm", [P, W_END])
        wfold = sb("wfold", [C, 320])
        bfirst = sb("bfirst", [C, P])
        wproj = sb("wproj", [P, 320])
        whigh = sb("whigh", [P, 320], F16)
        wlow = sb("wlow", [P, 320], F16)
        wog = [sb(f"wog{i}", [P, P], F16) for i in range(2)]
        cen = sb("cen", [P, P])
        small = sb("small", [P, 16])
        stats = sb("stats", [P, 4 * NCH, 6])
        unscale = small[:, 11:12]
        ones1 = sb("ones1", [1, P])
        eps1 = sb("eps1", [P, 1])
        epso = sb("epso", [P, 1])
        epsx = sb("epsx", [P, 1])

        banks = [ctx.enter_context(nc.psum_tensor(f"bank{i}", [P, GW], F32)) for i in range(4)]

        def bank(i):
            return banks[i // 2][:, (i % 2) * BANK:(i % 2 + 1) * BANK]

        loaded = [sem(f"loaded{i}") for i in range(2)]
        loaded_xh = [sem(f"loaded_xh{i}") for i in range(2)]
        loaded_xt = [sem(f"loaded_xt{i}") for i in range(2)]
        stored = [sem(f"stored{i}") for i in range(2)]
        prep = sem("prep")
        step = sem("step")
        enter_paired = sem("enter_paired")
        enter_turned = sem("enter_turned")
        enter_copied = sem("enter_copied")
        enter_counted = sem("enter_counted")
        centered = sem("centered")
        variance = sem("variance")
        squared = sem("squared")
        logged = sem("logged")
        rooted = sem("rooted")
        normed = sem("normed")
        centered_out = sem("centered_out")
        highs_ready = sem("highs_ready")
        lows_ready = sem("lows_ready")
        projected = sem("projected")
        gates_ready = sem("gates_ready")
        gates_masked = sem("gates_masked")
        products_ready = sem("products_ready")
        contracted = sem("contracted")
        copied = sem("copied")
        squares_ready = sem("squares_ready")
        summed = sem("summed")
        sums_cleared = sem("sums_cleared")
        turned = sem("turned")
        gate_projected = sem("gate_projected")
        out_projected = sem("out_projected")
        turned_back = sem("turned_back")
        scaled = sem("scaled")
        gate_ready = sem("gate_ready")
        tokens_ready = sem("tokens_ready")
        mean_off = sem("mean_off")
        gated_ready = sem("gated_ready")
        x_ready = sem("x_ready")
        stats_taken = sem("stats_taken")
        normalized = sem("normalized")
        tick = sem("tick")

        def advance(*counts):
            for sem_, n in counts:
                sem_.n += n

        K = lambda c, rows=P: kst[0:rows, c:c + P]
        vec = lambda i, rows=P: prm[0:rows, W_VEC + i:W_VEC + i + 1]

        with nc.Block() as block:
            @block.sync
            def _(sp):
                for s in sems:
                    sp.sem_inc(s.s, CREDIT)
                sp.dma_start(kst[:, :], consts).then_inc(prep.s, 16)
                sp.wait_ge(prep.s, prep.n + 16)

            @block.vector
            def _(dve):
                dve.memset(eps1[:, :], EPS)
                dve.memset(ones1[:, :], 1.0)
                dve.memset(epsx[:, :], EPS / X_SCALE ** 2)
        advance((prep, 16))

        def pair_chunk(dram, ut, vb):
            return dram[bass.ds(8 * ut, 8), :, bass.ds(vb * 256, 256)].rearrange("g p f -> p g f")

        def xh_chunk(n, part, rows, k_is_b):
            if k_is_b:
                return XH[bass.ds(n, 1), part, rows, :].rearrange("o p f -> p (o f)")
            return XHA[part, rows, :, bass.ds(8 * n, 8), :].rearrange("p t j a -> p t (j a)")

        def xh_cols(buf, k_is_b):
            return buf if k_is_b else buf.rearrange("p (t f) -> p t f", t=NT)

        def pair_cols(buf, q):
            return buf.rearrange("p (g f) -> p g f", g=8)[:, :, 64 * q:64 * q + 64]

        def by_b(buf, q):
            return buf.rearrange("p (j g r) -> p g j r", g=8, r=16)[:, :, 4 * q:4 * q + 4, :]

        def by_token_cols(buf, q):
            return pair_cols(buf, q).rearrange("p g (j r) -> p g j r", r=16)

        ar = Arena()
        e_n = [ar.take(COLS) for _ in range(2)]
        e_x = [ar.take(COLS) for _ in range(2)]
        e_t = [ar.take(COLS) for _ in range(2)]
        x_nat = x_in.rearrange("o (t a) (s v) c -> t (o a) s (v c)", t=NT, s=2)
        with nc.Block() as block:
            @block.sync
            def _(sp):
                with sp.Fori(0, NCH // 2) as i:
                    for h in range(2):
                        n = 2 * i + h
                        sp.wait_ge(enter_paired.s, enter_paired.n + n - 1)
                        sp.sem_inc(tick.s, 1)
                        ut, vb = i // 4, (2 * i + h) % 8
                        sp.dma_start(e_n[h].rearrange("p (s f) -> p s f", s=2),
                                     x_nat[ut, :, :, bass.ds(vb * 1024, 1024)]).then_inc(loaded[h].s, 16)
                for h in range(2):
                    sp.wait_ge(stored[h].s, stored[h].n + 8 * NCH)

            @block.tensor
            def _(pe):
                with pe.Fori(0, NCH // 2) as i:
                    for h in range(2):
                        pe.wait_ge(enter_paired.s, enter_paired.n + 2 * i + h + 1)
                        for q in range(4):
                            b = 4 * h + q
                            pe.wait_ge(enter_copied.s, enter_copied.n + 8 * i + b - 7)
                            for j in range(4):
                                last = pe.transpose(
                                    bank(b).rearrange("p (g j r) -> p g j r", g=8, j=4)[:, :, j, :],
                                    e_x[h][:, (4 * q + j) * P:(4 * q + j + 1) * P], K(K_IDENT))
                            last.then_inc(enter_turned.s, 1)

            @block.scalar
            def _(act):
                with act.Fori(0, NCH // 2) as i:
                    for h in range(2):
                        act.wait_ge(stored[h].s, stored[h].n + 16 * i)
                        act.wait_ge(enter_counted.s, enter_counted.n + 8 * i + 4 * h - 4)
                        for q in range(4):
                            act.wait_ge(enter_turned.s, enter_turned.n + 8 * i + 4 * h + q + 1)
                            act.activation(pair_cols(e_t[h], q),
                                           bank(4 * h + q).rearrange("p (g f) -> p g f", g=8),
                                           ACT.Copy).then_inc(enter_copied.s, 1)
                        act.wait_ge(enter_copied.s, enter_copied.n + 8 * i + 4 * h + 4)
                        ut, vb = i // 4, (2 * i + h) % 8
                        act.dma_start(pair_chunk(XT, ut, vb), e_t[h].rearrange("p (g f) -> p g f", g=8)) \
                            .then_inc(stored[h].s, 16)

            @block.vector
            def _(dve):
                def pair(i, k):
                    if k % 4 == 0:
                        h = k // 4
                        dve.wait_ge(loaded[h].s, loaded[h].n + 16 * i + 16)
                        dve.wait_ge(enter_turned.s, enter_turned.n + 8 * i + k - 4)
                        dve.tensor_copy(e_x[h].rearrange("p (v s c) -> p s v c", s=2, c=C),
                                        e_n[h].rearrange("p (s v c) -> p s v c", s=2, c=C)) \
                            .then_inc(enter_paired.s, 1)

                def count(i, k):
                    dve.wait_ge(enter_copied.s, enter_copied.n + 8 * i + k + 1)
                    dve.bn_stats(stats[:, bass.ds(8 * i + k, 1), :].rearrange("p o f -> p (o f)"),
                                 pair_cols(e_t[k // 4], k % 4)).then_inc(enter_counted.s, 1)

                pipeline(dve, NCH // 2, 8, (pair, 0), (count, 4))
        advance((loaded[0], 8 * NCH), (loaded[1], 8 * NCH), (stored[0], 8 * NCH), (stored[1], 8 * NCH),
                (enter_paired, NCH), (enter_turned, 4 * NCH), (enter_copied, 4 * NCH), (enter_counted, 4 * NCH))

        def prepare(number, layer):
            mean, var = small[:, 0:1], small[:, 1:2]
            dev, second, std, a, b, cb, most = (small[:, i:i + 1] for i in range(2, 9))
            scale = small[:, 10:11]
            wfold_p = squares[0][:, 0:320]
            w_cat = prm[0:C, W_CAT:W_CAT + 320]
            loads = 2 if layer["masked"] else 1
            with nc.Block() as block:
                @block.sync
                def _(sp):
                    sp.dma_start(prm[:, :], params[number]).then_inc(prep.s, 16)
                    if layer["masked"]:
                        sp.dma_start(mask_sb[:, :, :], masks[number // 2]).then_inc(prep.s, 16)

                @block.tensor
                def _(pe):
                    pe.wait_ge(step.s, step.n + 1)
                    pe.matmul(bank(0)[:, 0:1], K(K_GROUP), mean, start=True, stop=True).then_inc(step.s, 1)
                    pe.wait_ge(step.s, step.n + 5)
                    pe.matmul(bank(1)[:, 0:1], K(K_GROUP), second, start=True, stop=True).then_inc(step.s, 1)
                    pe.wait_ge(step.s, step.n + 11)
                    pe.matmul(bank(2)[:, 0:1], K(K_CENTER), b, start=True, stop=True).then_inc(step.s, 1)
                    pe.wait_ge(step.s, step.n + 15)
                    pe.matmul(bank(3)[:, 0:320], K(K_DROP, C), wfold[:, :], start=True, stop=False)
                    pe.matmul(bank(3)[:, 0:320], bfirst[:, :], w_cat, start=False, stop=False)
                    pe.matmul(bank(3)[:, 0:320], K(K_FIRST, 1), prm[0:1, W_BIAS:W_BIAS + 320],
                              start=False, stop=True).then_inc(step.s, 1)
                    pe.wait_ge(step.s, step.n + 21)
                    pe.transpose(bank(4)[0:1, 0:P], most, K(K_IDENT)).then_inc(step.s, 1)
                    pe.wait_ge(step.s, step.n + 23)
                    pe.matmul(bank(5)[:, 0:1], ones1[0:1, :], small[0:1, 9:10], start=True, stop=True) \
                        .then_inc(step.s, 1)

                @block.scalar
                def _(act):
                    act.wait_ge(step.s, step.n + 6)
                    act.activation(std, bank(1)[:, 0:1], ACT.Sqrt, bias=eps1[:, :]).then_inc(step.s, 1)
                    act.wait_ge(step.s, step.n + 19)
                    act.activation(wfold_p, wproj[:, :], ACT.Abs).then_inc(step.s, 1)

                @block.vector
                def _(dve):
                    dve.bn_aggr(small[:, 0:2], stats[:, :, :].rearrange("p t f -> p (t f)")).then_inc(step.s, 1)
                    dve.wait_ge(step.s, step.n + 2)
                    dve.tensor_tensor(dev, mean, bank(0)[:, 0:1], ALU.subtract).then_inc(step.s, 1)
                    dve.wait_ge(step.s, step.n + 3)
                    dve.tensor_tensor(second, dev, dev, ALU.mult).then_inc(step.s, 1)
                    dve.wait_ge(step.s, step.n + 4)
                    dve.tensor_tensor(second, second, var, ALU.add).then_inc(step.s, 1)
                    dve.wait_ge(step.s, step.n + 7)
                    dve.reciprocal(a, std).then_inc(step.s, 1)
                    dve.wait_ge(step.s, step.n + 8)
                    dve.tensor_tensor(b, a, bank(0)[:, 0:1], ALU.mult).then_inc(step.s, 1)
                    dve.wait_ge(step.s, step.n + 9)
                    dve.tensor_scalar(cen[:, :], K(K_CENTER), a, None, ALU.mult).then_inc(step.s, 1)
                    dve.wait_ge(step.s, step.n + 10)
                    dve.tensor_scalar(b, b, -1.0, None, ALU.mult).then_inc(step.s, 1)
                    dve.wait_ge(step.s, step.n + 12)
                    dve.tensor_copy(cb, bank(2)[:, 0:1]).then_inc(step.s, 1)
                    dve.wait_ge(prep.s, prep.n + 16 * loads)
                    dve.tensor_scalar(wfold[:, :], w_cat, vec(V_NW, C), None, ALU.mult).then_inc(step.s, 1)
                    dve.tensor_scalar(bfirst[:, :], K(K_FIRST, C), vec(V_NB, C), None, ALU.mult).then_inc(step.s, 1)
                    dve.memset(wog[0][:, :], 0.0).then_inc(step.s, 1)
                    dve.memset(wog[1][:, :], 0.0).then_inc(step.s, 1)
                    dve.wait_ge(step.s, step.n + 18)
                    dve.tensor_copy(wproj[:, :], bank(3)[:, 0:320]).then_inc(step.s, 1)
                    dve.wait_ge(step.s, step.n + 20)
                    dve.reduce_max(most, wfold_p, mybir.AxisListType.X).then_inc(step.s, 1)
                    dve.wait_ge(step.s, step.n + 22)
                    dve.reduce_max(small[0:1, 9:10], bank(4)[0:1, 0:P], mybir.AxisListType.X).then_inc(step.s, 1)
                    dve.wait_ge(step.s, step.n + 24)
                    dve.tensor_scalar(most, bank(5)[:, 0:1], 1e-30, 1.0 / W_SCALE, ALU.max, ALU.mult).then_inc(step.s, 1)
                    dve.wait_ge(step.s, step.n + 25)
                    dve.reciprocal(scale, most).then_inc(step.s, 1)
                    dve.wait_ge(step.s, step.n + 26)
                    dve.tensor_scalar(most, scale, X_SCALE, None, ALU.mult).then_inc(step.s, 1)
                    dve.tensor_scalar(wproj[:, :], wproj[:, :], scale, None, ALU.mult).then_inc(step.s, 1)
                    dve.wait_ge(step.s, step.n + 28)
                    dve.reciprocal(unscale, most).then_inc(step.s, 1)
                    dve.tensor_copy(whigh[:, :], wproj[:, :]).then_inc(step.s, 1)
                    dve.wait_ge(step.s, step.n + 30)
                    dve.tensor_tensor(wlow[:, :], wproj[:, :], whigh[:, :], ALU.subtract).then_inc(step.s, 1)
                    dve.wait_ge(step.s, step.n + 31)
                    for s in range(2):
                        for part, w in enumerate((whigh, wlow)):
                            dve.tensor_copy(wog[part][C * s:C * s + C, C * s:C * s + C],
                                            w[C * s:C * s + C, 256:320]).then_inc(step.s, 1)
            advance((prep, 16 * loads), (step, 35))

        def norm(number, layer):
            ar = Arena()
            xa = [ar.take(COLS) for _ in range(2)]
            high = [ar.take(COLS // 2).bitcast(F16) for _ in range(2)]
            low = [ar.take(COLS // 2).bitcast(F16) for _ in range(2)]
            sq, yc, lnv, rs = ([ar.take(GW) for _ in range(k)] for k in (2, 4, 2, 4))
            cb, k_is_b = small[:, 7:8], layer["k_is_b"]
            keep, one = kst[:, K_KEEP:K_KEEP + 1], kst[:, K_ONE:K_ONE + 1]
            with nc.Block() as block:
                @block.sync
                def _(sp):
                    def load(n, h):
                        if k_is_b:
                            sp.dma_start(xa[h], XT[bass.ds(n, 1), :, :].rearrange("o p f -> p (o f)")) \
                                .then_inc(loaded[h].s, 16)
                        else:
                            sp.dma_start(xa[h].rearrange("p (g f) -> p g f", g=16),
                                         XT[:, :, bass.ds(n * 128, 128)].rearrange("g p f -> p g f")) \
                                .then_inc(loaded[h].s, 16)

                    def store(n, h):
                        sp.wait_ge(lows_ready.s, lows_ready.n + 2 * n + 2)
                        sp.sem_inc(tick.s, 1)
                        for part, v in enumerate((high[h], low[h])):
                            sp.dma_start(xh_chunk(n, part, slice(0, P), k_is_b), xh_cols(v, k_is_b)) \
                                .then_inc(stored[h].s, 16)

                    for h in range(2):
                        load(h, h)
                    with sp.Fori(0, NCH // 2 - 1) as i:
                        for h in range(2):
                            sp.wait_ge(centered.s, centered.n + 4 * i + 2 * h + 2)
                            sp.sem_inc(tick.s, 1)
                            load(2 * i + h + 2, h)
                            store(2 * i + h, h)
                    for h in range(2):
                        store(NCH - 2 + h, h)
                    for h in range(2):
                        sp.wait_ge(stored[h].s, stored[h].n + 16 * NCH)

                @block.tensor
                def _(pe):
                    def center(i, k):
                        h, t = divmod(k, 2)
                        if t == 0:
                            pe.wait_ge(loaded[h].s, loaded[h].n + 16 * i + 16)
                        pe.wait_ge(centered_out.s, centered_out.n + 4 * i + k - 1)
                        for u in range(2):
                            at = 2 * t + u
                            cols = xa[h][:, at * BANK:(at + 1) * BANK] if k_is_b else \
                                xa[h].rearrange("p (g j r) -> p j g r", g=16, j=8)[
                                    :, 4 * (at % 2):4 * (at % 2) + 4, 8 * (at // 2):8 * (at // 2) + 8, :]
                            last = pe.matmul(banks[k % 2][:, u * BANK:(u + 1) * BANK], cen[:, :], cols,
                                             start=True, stop=True)
                        last.then_inc(centered.s, 1)

                    def vary(i, k):
                        pe.wait_ge(squared.s, squared.n + 4 * i + k + 1)
                        pe.wait_ge(logged.s, logged.n + 4 * i + k - 1)
                        for u in range(2):
                            last = pe.matmul(banks[2 + k % 2][:, u * BANK:(u + 1) * BANK], K(K_MEAN),
                                             sq[k % 2][:, u * BANK:(u + 1) * BANK], start=True, stop=True)
                        last.then_inc(variance.s, 1)

                    pipeline(pe, NCH // 2, 4, (center, 0), (vary, 1))

                @block.scalar
                def _(act):
                    def square(i, k):
                        act.wait_ge(centered.s, centered.n + 4 * i + k + 1)
                        act.wait_ge(variance.s, variance.n + 4 * i + k - 1)
                        act.activation(sq[k % 2], banks[k % 2][:, :], ACT.Square, bias=cb).then_inc(squared.s, 1)

                    def root(i, k):
                        act.wait_ge(variance.s, variance.n + 4 * i + k + 1)
                        act.wait_ge(rooted.s, rooted.n + 4 * i + k - 1)
                        act.activation(lnv[k % 2], banks[2 + k % 2][:, :], ACT.Ln, bias=epsx[:, :],
                                       scale=1.0 / X_SCALE ** 2).then_inc(logged.s, 1)
                        act.wait_ge(logged.s, logged.n + 4 * i + k + 1)
                        act.wait_ge(normed.s, normed.n + 4 * i + k - 3)
                        act.activation(rs[k], lnv[k % 2], ACT.Exp, scale=-0.5).then_inc(rooted.s, 1)

                    act.preload_act_table_set("natural_log_exp_and_others")
                    pipeline(act, NCH // 2, 4, (square, 0), (root, 1))

                @block.gpsimd
                def _(pool):
                    def multiply(i, k):
                        pool.wait_ge(rooted.s, rooted.n + 4 * i + k + 1)
                        pool.wait_ge(centered_out.s, centered_out.n + 4 * i + k + 1)
                        pool.tensor_tensor(yc[k], yc[k], rs[k], ALU.mult).then_inc(normed.s, 1)

                    pipeline(pool, NCH // 2, 4, (multiply, 0))

                @block.vector
                def _(dve):
                    def copy_out(i, k):
                        dve.wait_ge(squared.s, squared.n + 4 * i + k + 1)
                        dve.wait_ge(lows_ready.s, lows_ready.n + 4 * i + k - 3)
                        dve.tensor_scalar(yc[k], banks[k % 2][:, :], cb, keep, ALU.add, ALU.mult) \
                            .then_inc(centered_out.s, 1)

                    def split(i, k):
                        h, cols = k // 2, slice((k % 2) * GW, (k % 2 + 1) * GW)
                        dve.wait_ge(normed.s, normed.n + 4 * i + k + 1)
                        if k % 2 == 0:
                            dve.wait_ge(stored[h].s, stored[h].n + 32 * i)
                        dve.tensor_scalar(high[h][:, cols], yc[k], one, None, ALU.add).then_inc(highs_ready.s, 1)
                        dve.wait_ge(highs_ready.s, highs_ready.n + 4 * i + k + 1)
                        dve.scalar_tensor_tensor(low[h][:, cols], yc[k], one, high[h][:, cols],
                                                 ALU.add, ALU.subtract).then_inc(lows_ready.s, 1)

                    pipeline(dve, NCH // 2, 4, (copy_out, 0), (split, 2))
            advance((loaded[0], 8 * NCH), (loaded[1], 8 * NCH), (stored[0], 16 * NCH), (stored[1], 16 * NCH),
                    (centered, 2 * NCH), (variance, 2 * NCH), (squared, 2 * NCH), (logged, 2 * NCH),
                    (rooted, 2 * NCH), (normed, 2 * NCH), (centered_out, 2 * NCH), (highs_ready, 2 * NCH),
                    (lows_ready, 2 * NCH))

        def project(number, layer, half):
            k_is_b, masked = layer["k_is_b"], layer["masked"]
            dest = LRb if layer["low"] else LR
            gate = msg if masked else sig
            used, gates = (gates_masked, gates_masked) if masked else (products_ready, gates_ready)

            def where(n, g):
                if k_is_b:
                    return g // 2, 16 * n + 8 * (g % 2)
                return g % 2, P * (g // 2) + 8 * n

            with nc.Block() as block:
                @block.sync
                def _(sp):
                    with sp.Fori(0, NCH // 2) as i:
                        for h in range(2):
                            n = 2 * i + h
                            sp.wait_ge(projected.s, projected.n + 4 * n - 4)
                            sp.sem_inc(tick.s, 1)
                            for s in range(2):
                                for part in range(2):
                                    sp.dma_start(xh_cols(xh_b[h][s][C * part:C * part + C, :], k_is_b),
                                                 xh_chunk(n, part, slice(C * s, C * s + C), k_is_b)) \
                                        .then_inc(loaded[h].s, 16)

                @block.tensor
                def _(pe):
                    with pe.Fori(0, NCH // 2) as i:
                        for h in range(2):
                            pe.wait_ge(loaded[h].s, loaded[h].n + 64 * i + 64)
                            for g in range(4):
                                pe.wait_ge(products_ready.s, products_ready.n + 8 * i + 4 * h + g - 3)
                                for j in range(8):
                                    x = xh_b[h][g // 2]
                                    if k_is_b:
                                        tokens = x.rearrange("p (b r) -> p b r", r=16)[:, :, 8 * (g % 2) + j]
                                    else:
                                        tokens = x[:, (8 * (g % 2) + j) * P:(8 * (g % 2) + j + 1) * P]
                                    for part, w in enumerate((whigh, wlow)):
                                        last = pe.matmul(banks[g][:, j * P:(j + 1) * P], tokens,
                                                         w[:, half * P:(half + 1) * P], start=part == 0, stop=part == 1)
                                last.then_inc(projected.s, 1)

                @block.scalar
                def _(act):
                    act.preload_act_table_set("sigmoid_and_others")
                    with act.Fori(0, NCH // 2) as i:
                        for h in range(2):
                            for g in range(4):
                                group = 8 * i + 4 * h + g
                                act.wait_ge(projected.s, projected.n + group + 1)
                                act.wait_ge(used.s, used.n + group - 1)
                                act.activation(sig[g % 2][:, :, :],
                                               banks[g][:, :].rearrange("p (m c) -> p c m", m=8)[:, C:, :],
                                               ACT.Sigmoid, scale=unscale).then_inc(gates_ready.s, 1)

                if masked:
                    @block.gpsimd
                    def _(pool):
                        with pool.Fori(0, NCH // 2) as i:
                            for h in range(2):
                                for g in range(4):
                                    group = 8 * i + 4 * h + g
                                    kt, m = where(2 * i + h, g)
                                    pool.wait_ge(gates_ready.s, gates_ready.n + group + 1)
                                    pool.wait_ge(products_ready.s, products_ready.n + group - 1)
                                    pool.tensor_tensor(msg[g % 2][:, :, :], sig[g % 2][:, :, :],
                                                       mask_sb[:, kt, bass.ds(m, 8)].unsqueeze(1).broadcast_to([P, C, 8]),
                                                       ALU.mult).then_inc(gates_masked.s, 1)

                @block.vector
                def _(dve):
                    with dve.Fori(0, NCH // 2) as i:
                        for h in range(2):
                            for g in range(4):
                                kt, m = where(2 * i + h, g)
                                dve.wait_ge(gates.s, gates.n + 8 * i + 4 * h + g + 1)
                                dve.scalar_tensor_tensor(dest[:, kt, :, bass.ds(m, 8)],
                                                         banks[g][:, :].rearrange("p (m c) -> p c m", m=8)[:, 0:C, :],
                                                         unscale, gate[g % 2][:, :, :], ALU.mult, ALU.mult) \
                                    .then_inc(products_ready.s, 1)
            advance((loaded[0], 32 * NCH), (loaded[1], 32 * NCH), (projected, 4 * NCH), (gates_ready, 4 * NCH),
                    (products_ready, 4 * NCH))
            if masked:
                advance((gates_masked, 4 * NCH))

        def contract(number, layer, half):
            low = layer["low"]
            src = LRb if low else LR
            off_a, off_b = (0, HALF) if layer["left_a"] else (HALF, 0)
            hold = [(o[:, :].bitcast(BF16)[:, 0:16 * 256] if low else o[:, :]) for o in obuf]
            by_block = [o.rearrange("p (v c r) -> p v c r", v=16, c=16) for o in hold]
            by_channel = [o.rearrange("p (v c r) -> p c v r", v=16, c=16) for o in hold]
            parts = [(piece, g) for piece in range(4) for g in range(4)]
            with nc.Block() as block:
                @block.tensor
                def _(pe):
                    for e, (piece, g) in enumerate(parts):
                        cq, ut = divmod(piece, 2)
                        if e >= 4:
                            pe.wait_ge(copied.s, copied.n + e - 3)
                        for c in range(4):
                            ch = 16 * cq + 4 * g + c
                            for kt in range(NT):
                                last = pe.matmul(banks[e % 4][:, c * N:(c + 1) * N],
                                                 src[:, kt, off_a + ch, ut * P:(ut + 1) * P],
                                                 src[:, kt, off_b + ch, :], start=kt == 0, stop=kt == NT - 1)
                        last.then_inc(contracted.s, 1)

                @block.scalar
                def _(act):
                    for e, (piece, g) in enumerate(parts):
                        if piece >= 2 and g == 0:
                            act.wait_ge(stored[piece % 2].s, stored[piece % 2].n + 16)
                            act.wait_ge(summed.s, summed.n + 4 * 4 * (piece - 1))
                        act.wait_ge(contracted.s, contracted.n + e + 1)
                        act.activation(by_channel[piece % 2][:, 4 * g:4 * g + 4, :, :],
                                       banks[e % 4][:, :].rearrange("p (c v r) -> p c v r", c=4, r=16),
                                       ACT.Copy).then_inc(copied.s, 1)
                        act.wait_ge(copied.s, copied.n + e + 1)
                        if e >= 2:
                            act.wait_ge(summed.s, summed.n + 4 * (e - 1))
                        act.activation(squares[e % 2][:, :].rearrange("p (c v r) -> p c v r", c=4, r=16),
                                       by_channel[piece % 2][:, 4 * g:4 * g + 4, :, :],
                                       ACT.Square).then_inc(squares_ready.s, 1)

                @block.vector
                def _(dve):
                    if half == 0:
                        dve.memset(sum1[:, :, :], 0.0).then_inc(sums_cleared.s, 1)
                        dve.memset(sum2[:, :, :], 0.0).then_inc(sums_cleared.s, 1)
                        dve.wait_ge(sums_cleared.s, sums_cleared.n + 2)
                    for e, (piece, g) in enumerate(parts):
                        ut = piece % 2
                        for two in range(2):
                            if two == 0:
                                dve.wait_ge(copied.s, copied.n + e + 1)
                            if e or two:
                                dve.wait_ge(summed.s, summed.n + 4 * e + 2 * two - 1)
                            dve.tensor_tensor(sum1[:, ut, :].rearrange("p (c v r) -> p c v r", c=2, r=16),
                                              sum1[:, ut, :].rearrange("p (c v r) -> p c v r", c=2, r=16),
                                              by_channel[piece % 2][:, 4 * g + 2 * two:4 * g + 2 * two + 2, :, :],
                                              ALU.add).then_inc(summed.s, 1)
                            if two == 0:
                                dve.wait_ge(squares_ready.s, squares_ready.n + e + 1)
                            if e or two:
                                dve.wait_ge(summed.s, summed.n + 4 * e + 2 * two)
                            dve.tensor_tensor(sum2[:, ut, :], sum2[:, ut, :],
                                              squares[e % 2][:, 2 * two * N:2 * (two + 1) * N],
                                              ALU.add).then_inc(summed.s, 1)

                @block.sync
                def _(sp):
                    for piece in range(4):
                        cq, ut = divmod(piece, 2)
                        sp.wait_ge(copied.s, copied.n + 4 * (piece + 1))
                        sp.dma_start((OSL if low else OS)[ut, :, 2 * half + cq, :, :].rearrange("v p f -> p v f"),
                                     hold[piece % 2].rearrange("p (v f) -> p v f", v=16)) \
                            .then_inc(stored[piece % 2].s, 16)
                    for h in range(2):
                        sp.wait_ge(stored[h].s, stored[h].n + 32)
            advance((contracted, 16), (copied, 16), (squares_ready, 16), (summed, 64), (stored[0], 32), (stored[1], 32))
            if half == 0:
                advance((sums_cleared, 2))

        def moments(number, layer):
            s1 = [sum1[:, :, i * N:(i + 1) * N] for i in range(2)]
            s2 = [sum2[:, :, i * N:(i + 1) * N] for i in range(2)]
            with nc.Block() as block:
                @block.vector
                def _(dve):
                    at = [0]

                    def then(ins):
                        at[0] += 1
                        ins.then_inc(step.s, 1)
                        dve.wait_ge(step.s, step.n + at[0])

                    then(dve.memset(epso[:, :], EPS * layer["div"] ** 2))
                    then(dve.tensor_tensor(s1[0], s1[0], s1[1], ALU.add))
                    then(dve.tensor_scalar(s1[0], s1[0], 1.0 / C, None, ALU.mult))
                    then(dve.tensor_tensor(s2[0], s2[0], s2[1], ALU.add))
                    then(dve.tensor_tensor(s1[1], s1[0], s1[0], ALU.mult))
                    then(dve.scalar_tensor_tensor(s2[0], s2[0], 1.0 / C, s1[1], ALU.mult, ALU.subtract))
                    dve.tensor_scalar(s2[0], s2[0], 0.0, None, ALU.max).then_inc(step.s, 1)
                    dve.wait_ge(step.s, step.n + 8)
                    dve.reciprocal(s2[0], s2[1]).then_inc(step.s, 1)

                @block.scalar
                def _(act):
                    act.wait_ge(step.s, step.n + 7)
                    act.activation(s2[1], s2[0], ACT.Sqrt, bias=epso[:, :]).then_inc(step.s, 1)
            advance((step, 9))

        def finish(number, layer):
            low, gate_first, end = layer["low"], layer["gate_first"], number == len(LAYERS) - 1
            k_is_b = layer["k_is_b"]
            ar = Arena()
            o_in, nrm, xi, xo, nat = ([ar.take(COLS) for _ in range(2)] for _ in range(5))
            xh = [[ar.take(COLS // 2).bitcast(F16) for _ in range(2)] for _ in range(2)]
            aff, og, gated = ([ar.take(BANK) for _ in range(4)] for _ in range(3))
            o_f = [o.bitcast(BF16)[:, 0:COLS] if low else o for o in o_in]
            o_v = [o.rearrange("p (s c v) -> p s c v", s=2, c=C) for o in o_f]
            n_v = [o.rearrange("p (v s c) -> p s c v", s=2, c=C) for o in nrm]
            w_out = prm[:, W_OUT:W_OUT + P]
            out_nat = out.rearrange("o (t a) (s v) c -> t (o a) s (v c)", t=NT, s=2)
            fed, taken, aff_used = (gated_ready, x_ready, gated_ready) if gate_first else (scaled, gated_ready, out_projected)
            rounds = NCH // 2

            def at(i, h):
                return i // 4, (2 * i + h) % 8

            def token(t, i, h):
                ut, vb = at(i, h)
                v = t[:, bass.ds(ut, 1), 0:N].rearrange("p o (s v) -> p (o s) v", s=2)[:, :, bass.ds(16 * vb, 16)]
                return v.unsqueeze(2).broadcast_to([P, 2, C, 16])

            def tall(v):
                return v.rearrange("p (g f) -> p g f", g=8)

            def by_token(v):
                return v.rearrange("p (g j r) -> p g j r", g=8, j=4)

            with nc.Block() as block:
                @block.sync
                def _(sp):
                    def load_os(i, h):
                        ut, vb = at(i, h)
                        for s in range(2):
                            sp.dma_start(o_f[h][:, s * 1024:(s + 1) * 1024].rearrange("p (q f) -> p q f", q=4),
                                         (OSL if low else OS)[bass.ds(ut, 1), bass.ds(8 * s + vb, 1)]
                                         .rearrange("t o q p f -> p (t o q) f")).then_inc(loaded[h].s, 16)

                    def load_xh(i, h):
                        ut, vb = at(i, h)
                        for part in range(2):
                            if k_is_b:
                                sp.dma_start(tall(xh[h][part]),
                                             XH[bass.ds(8 * ut, 8), part, :, bass.ds(vb * 256, 256)]
                                             .rearrange("g p f -> p g f")).then_inc(loaded_xh[h].s, 16)
                            else:
                                sp.dma_start(xh[h][part].rearrange("p (t f) -> p t f", t=1),
                                             XHA[part, :, bass.ds(ut, 1), bass.ds(16 * vb, 16), :]
                                             .rearrange("p t j a -> p t (j a)")).then_inc(loaded_xh[h].s, 16)

                    def load_xt(i, h):
                        ut, vb = at(i, h)
                        sp.dma_start(tall(xi[h]), pair_chunk(XT, ut, vb)).then_inc(loaded_xt[h].s, 16)

                    def store(i, h):
                        ut, vb = at(i, h)
                        if end:
                            sp.wait_ge(tokens_ready.s, tokens_ready.n + 8 * i + 4 * h + 4)
                            sp.sem_inc(tick.s, 1)
                            sp.dma_start(out_nat[bass.ds(ut, 1), :, :, bass.ds(vb * 1024, 1024)]
                                         .rearrange("t a s f -> a (t s) f"),
                                         nat[h].rearrange("p (s f) -> p s f", s=2)).then_inc(stored[h].s, 16)
                        else:
                            sp.wait_ge(x_ready.s, x_ready.n + 8 * i + 4 * h + 4)
                            sp.sem_inc(tick.s, 1)
                            sp.dma_start(pair_chunk(XT, ut, vb), tall(xo[h])).then_inc(stored[h].s, 16)

                    for h in range(2):
                        load_os(0, h)
                        load_xh(0, h)
                        load_xt(0, h)
                    with sp.Fori(0, rounds - 1) as i:
                        for h in range(2):
                            sp.wait_ge(mean_off.s, mean_off.n + 2 * i + h + 1)
                            sp.sem_inc(tick.s, 1)
                            load_os(i + 1, h)
                            sp.wait_ge(gate_projected.s, gate_projected.n + 8 * i + 4 * h + 4)
                            sp.sem_inc(tick.s, 1)
                            load_xh(i + 1, h)
                            sp.wait_ge(x_ready.s, x_ready.n + 8 * i + 4 * h + 4)
                            sp.sem_inc(tick.s, 1)
                            load_xt(i + 1, h)
                            store(i, h)
                    for h in range(2):
                        store(rounds - 1, h)
                    for h in range(2):
                        sp.wait_ge(stored[h].s, stored[h].n + 8 * NCH)

                @block.tensor
                def _(pe):
                    def turn(i, k):
                        h, q = divmod(k, 4)
                        tile = 8 * i + k
                        if q == 0:
                            pe.wait_ge(normalized.s, normalized.n + 2 * i + h + 1)
                        pe.wait_ge(scaled.s, scaled.n + tile - 1)
                        for j in range(4):
                            last = pe.transpose(by_token(bank(k % 2))[:, :, j, :],
                                                nrm[h][:, (4 * q + j) * P:(4 * q + j + 1) * P], K(K_IDENT))
                        last.then_inc(turned.s, 1)

                    def out_gate(i, k):
                        h, q = divmod(k, 4)
                        if q == 0:
                            pe.wait_ge(loaded_xh[h].s, loaded_xh[h].n + 32 * i + 32)
                        pe.wait_ge(gate_ready.s, gate_ready.n + 8 * i + k - 1)
                        for w, part in ((0, 0), (0, 1), (1, 0)):
                            x = xh[h][part]
                            last = pe.matmul(bank(2 + k % 2), wog[w][:, :], pair_cols(x, q) if k_is_b else by_b(x, q),
                                             start=(w, part) == (0, 0), stop=w == 1)
                        last.then_inc(gate_projected.s, 1)

                    def project_out(i, k):
                        tile = 8 * i + k
                        pe.wait_ge(fed.s, fed.n + tile + 1)
                        pe.wait_ge(taken.s, taken.n + tile - 1)
                        pe.matmul(bank(4 + k % 2), w_out, (gated if gate_first else aff)[k % 4],
                                  start=True, stop=True).then_inc(out_projected.s, 1)

                    def turn_back(i, k):
                        h, q = divmod(k, 4)
                        tile = 8 * i + k
                        pe.wait_ge(x_ready.s, x_ready.n + tile + 1)
                        pe.wait_ge(tokens_ready.s, tokens_ready.n + tile - 1)
                        for j in range(4):
                            last = pe.transpose(bank(6 + k % 2)[:, j * P:(j + 1) * P],
                                                xo[h][:, (4 * q + j) * P:(4 * q + j + 1) * P], K(K_IDENT))
                        last.then_inc(turned_back.s, 1)

                    pipeline(pe, rounds, 8, (turn, 0), (out_gate, 0), (project_out, 1 if not gate_first else 2),
                             *([(turn_back, 4)] if end else []))

                @block.scalar
                def _(act):
                    def scale_shift(i, k):
                        tile = 8 * i + k
                        act.wait_ge(turned.s, turned.n + tile + 1)
                        act.wait_ge(aff_used.s, aff_used.n + tile - 3)
                        act.activation(aff[k % 4], bank(k % 2), ACT.Identity, bias=vec(V_OB),
                                       scale=vec(V_OW)).then_inc(scaled.s, 1)

                    def sigmoid(i, k):
                        tile = 8 * i + k
                        act.wait_ge(gate_projected.s, gate_projected.n + tile + 1)
                        act.wait_ge(gated_ready.s, gated_ready.n + tile - 3)
                        act.activation(og[k % 4], bank(2 + k % 2), ACT.Sigmoid, scale=unscale).then_inc(gate_ready.s, 1)

                    def back(i, k):
                        h, q = divmod(k, 4)
                        if q == 0:
                            act.wait_ge(stored[h].s, stored[h].n + 16 * i)
                        act.wait_ge(turned_back.s, turned_back.n + 8 * i + k + 1)
                        act.activation(nat[h].rearrange("p (s v c) -> p v s c", s=2, c=C)[:, 4 * q:4 * q + 4, :, :],
                                       bank(6 + k % 2).rearrange("p (j s c) -> p j s c", j=4, s=2),
                                       ACT.Copy).then_inc(tokens_ready.s, 1)

                    act.preload_act_table_set("sigmoid_and_others")
                    pipeline(act, rounds, 8, (scale_shift, 0), (sigmoid, 0), *([(back, 4)] if end else []))

                @block.gpsimd
                def _(pool):
                    def normalize(i, k):
                        if k % 4 == 0:
                            h = k // 4
                            pool.wait_ge(mean_off.s, mean_off.n + 2 * i + h + 1)
                            pool.tensor_tensor(n_v[h], n_v[h], token(sum2, i, h), ALU.mult).then_inc(normalized.s, 1)

                    def add(i, k):
                        h, q = divmod(k, 4)
                        if q == 0:
                            pool.wait_ge(loaded_xt[h].s, loaded_xt[h].n + 16 * i + 16)
                            if not end:
                                pool.wait_ge(stored[h].s, stored[h].n + 16 * i)
                        if end:
                            pool.wait_ge(turned_back.s, turned_back.n + 8 * i + k - 7)
                        else:
                            pool.wait_ge(stats_taken.s, stats_taken.n + 8 * i + k - 7)
                        pool.wait_ge(gated_ready.s, gated_ready.n + 8 * i + k + 1)
                        pool.tensor_tensor(by_b(xo[h], q) if end else by_token_cols(xo[h], q),
                                           by_token(gated[k % 4]), by_token_cols(xi[h], q),
                                           ALU.add).then_inc(x_ready.s, 1)

                    if gate_first:
                        pipeline(pool, rounds, 8, (normalize, 0))
                    else:
                        pipeline(pool, rounds, 8, (normalize, 0), (add, 5))

                @block.vector
                def _(dve):
                    def center(i, k):
                        if k % 4 == 0:
                            h = k // 4
                            dve.wait_ge(loaded[h].s, loaded[h].n + 32 * i + 32)
                            dve.wait_ge(turned.s, turned.n + 8 * i + k - 4)
                            dve.tensor_tensor(n_v[h], o_v[h], token(sum1, i, h), ALU.subtract).then_inc(mean_off.s, 1)

                    def gate(i, k):
                        tile = 8 * i + k
                        dve.wait_ge(scaled.s, scaled.n + tile + 1)
                        dve.wait_ge(gate_ready.s, gate_ready.n + tile + 1)
                        dve.wait_ge(out_projected.s, out_projected.n + tile - 3)
                        dve.tensor_tensor(gated[k % 4], aff[k % 4], og[k % 4], ALU.mult).then_inc(gated_ready.s, 1)

                    def add(i, k):
                        h, q = divmod(k, 4)
                        if q == 0:
                            dve.wait_ge(loaded_xt[h].s, loaded_xt[h].n + 16 * i + 16)
                            dve.wait_ge(stored[h].s, stored[h].n + 16 * i)
                        dve.wait_ge(out_projected.s, out_projected.n + 8 * i + k + 1)
                        dve.scalar_tensor_tensor(pair_cols(xo[h], q), tall(bank(4 + k % 2)), vec(V_BO),
                                                 pair_cols(xi[h], q), ALU.add, ALU.add).then_inc(x_ready.s, 1)

                    def gate_late(i, k):
                        tile = 8 * i + k
                        dve.wait_ge(out_projected.s, out_projected.n + tile + 1)
                        dve.wait_ge(gate_ready.s, gate_ready.n + tile + 1)
                        dve.wait_ge(x_ready.s, x_ready.n + tile - 3)
                        dve.scalar_tensor_tensor(gated[k % 4], bank(4 + k % 2), vec(V_BO), og[k % 4],
                                                 ALU.add, ALU.mult).then_inc(gated_ready.s, 1)

                    def count(i, k):
                        h, q = divmod(k, 4)
                        dve.wait_ge(x_ready.s, x_ready.n + 8 * i + k + 1)
                        dve.bn_stats(stats[:, bass.ds(8 * i + k, 1), :].rearrange("p o f -> p (o f)"),
                                     pair_cols(xo[h], q)).then_inc(stats_taken.s, 1)

                    if gate_first:
                        pipeline(dve, rounds, 8, (center, 0), (gate, 4), (add, 6), (count, 7))
                    elif end:
                        pipeline(dve, rounds, 8, (center, 0), (gate_late, 4))
                    else:
                        pipeline(dve, rounds, 8, (center, 0), (gate_late, 4), (count, 6))
            advance((loaded[0], 16 * NCH), (loaded[1], 16 * NCH), (loaded_xh[0], 16 * NCH), (loaded_xh[1], 16 * NCH),
                    (loaded_xt[0], 8 * NCH), (loaded_xt[1], 8 * NCH), (stored[0], 8 * NCH), (stored[1], 8 * NCH),
                    (turned, 4 * NCH), (gate_projected, 4 * NCH), (out_projected, 4 * NCH), (scaled, 4 * NCH),
                    (gate_ready, 4 * NCH), (mean_off, NCH), (gated_ready, 4 * NCH), (x_ready, 4 * NCH),
                    (normalized, NCH))
            if end:
                advance((turned_back, 4 * NCH), (tokens_ready, 4 * NCH))
            else:
                advance((stats_taken, 4 * NCH))

        for number, layer in enumerate(LAYERS):
            prepare(number, layer)
            norm(number, layer)
            for half in range(2):
                project(number, layer, half)
                contract(number, layer, half)
            moments(number, layer)
            finish(number, layer)


def constants():
    import numpy as np

    k = np.zeros((P, K_END), np.float32)
    same_half = np.arange(P)[:, None] // C == np.arange(P)[None, :] // C
    channel = np.arange(P) % C
    k[:, K_CENTER:K_CENTER + P] = np.eye(P) - same_half / C
    k[:, K_MEAN:K_MEAN + P] = same_half / C
    k[:, K_GROUP:K_GROUP + P] = (channel[:, None] // 2 == channel[None, :] // 2) / 4
    k[:, K_IDENT:K_IDENT + P] = np.eye(P)
    drop = (channel[:C, None] == channel[None, :]).astype(np.float32)
    drop[0, :] = -1
    drop[:, channel == 0] = 0
    k[:C, K_DROP:K_DROP + P] = drop
    k[:, K_FIRST:K_FIRST + P] = channel[None, :] == 0
    k[:, K_KEEP] = channel != 0
    k[:, K_ONE] = X_SCALE * (channel == 0)
    return k


def pack(wl, wr, wlg, wrg, wog, wo, biases, nw, nb, ow, ob, bo):
    import numpy as np

    p = np.zeros((P, W_END), np.float32)
    order = [(m, h) for h in range(2) for m in range(4)]
    mats, vecs = [wl, wr, wlg, wrg], biases[:4]
    for i, (m, h) in enumerate(order):
        p[:C, W_CAT + 32 * i:W_CAT + 32 * i + 32] = mats[m][:, HALF * h:HALF * h + HALF]
        if vecs[m] is not None:
            p[0, W_BIAS + 32 * i:W_BIAS + 32 * i + 32] = vecs[m][HALF * h:HALF * h + HALF]
    p[:C, W_CAT + 256:W_CAT + 320] = wog
    if biases[4] is not None:
        p[0, W_BIAS + 256:W_BIAS + 320] = biases[4]
    for s in range(2):
        p[C * s:C * s + C, W_OUT + C * s:W_OUT + C * s + C] = wo
        for i, v in enumerate((nw, nb, ow, ob, bo)):
            if v is not None:
                p[C * s:C * s + C, W_VEC + i] = v
    return p


def kernel(**inputs):
    import numpy as np
    import concourse.bacc as bacc
    from concourse.bass_utils import run_bass_kernel_spmd as run

    a = {k: np.asarray(v) for k, v in inputs.items()}
    l0 = {k[8:]: v for k, v in a.items() if k.startswith("L0_conv_")}
    l1 = {k[8:]: v for k, v in a.items() if k.startswith("L1_conv_")}
    l2 = {k[8:]: v for k, v in a.items() if k.startswith("L2_conv_")}
    l3 = {k[8:]: v for k, v in a.items() if k.startswith("L3_conv_")}
    params = np.stack([
        pack(l0["w_left"].T, l0["w_right"].T, l0["w_lgate"].T, l0["w_rgate"].T, l0["w_ogate"].T, l0["w_out"].T,
             [None] * 5, l0["norm_w"], l0["norm_b"], l0["onorm_w"], l0["onorm_b"], None),
        pack(l1["Wl"], l1["Wr"], l1["Wlg"], l1["Wrg"], l1["Wog"], l1["Wo"],
             [l1["bl"], l1["br"], l1["blg"], l1["brg"], l1["bog"]],
             l1["norm_a"], l1["norm_b"], l1["on_a"], l1["on_b"], l1["bo"]),
        pack(l2["w_a_p"], l2["w_b_p"], l2["w_a_g"], l2["w_b_g"], l2["w_g"], l2["w_z"],
             [l2["b_a_p"], l2["b_b_p"], l2["b_a_g"], l2["b_b_g"], l2["b_g"]],
             l2["ln_in_scale"], l2["ln_in_bias"], l2["ln_out_scale"], l2["ln_out_bias"], l2["b_z"]),
        pack(l3["Wl"], l3["Wr"], l3["Wlg"], l3["Wrg"], l3["Wog"], l3["Wo"],
             [l3["bl"], l3["br"], l3["blg"], l3["brg"], l3["bog"]],
             l3["ln_in_g"], l3["ln_in_b"], l3["ln_out_g"], l3["ln_out_b"], l3["bo"]),
    ])
    masks = np.stack([np.ascontiguousarray(m[0].T.reshape(NT, P, N).transpose(1, 0, 2))
                      for m in (l0["mask"], l2["mask"])])
    arrays = {"x": np.ascontiguousarray(a["x"]), "masks": masks, "consts": constants(), "params": params}
    nc = bacc.Bacc("TRN2", target_bir_lowering=False, num_devices=1)
    aps = [nc.dram_tensor(name, v.shape, F32, kind="ExternalInput").ap() for name, v in arrays.items()]
    out = nc.dram_tensor("out", a["x"].shape, F32, kind="ExternalOutput").ap()
    build(nc, *aps, out)
    return run(nc, [arrays], core_ids=[0]).results[0]["out"]
```

```python
from contextlib import ExitStack

import concourse.bass as bass
from concourse import mybir

F32 = mybir.dt.float32
BF16 = mybir.dt.bfloat16
F16 = mybir.dt.float16
ALU = mybir.AluOpType
ACT = mybir.ActivationFunctionType

P = 128
N = 256
C = 64
HALF = 32
NT = N // P
BLK = 16
COLS = 2048
NCH = N * N // 2 // COLS
BANK = 512
EPS = 1e-5
GW = 2 * BANK
X_SCALE = 1024.0
W_SCALE = 1024.0
CREDIT = 64

LAYERS = [
    dict(k_is_b=True, masked=True, low=True, left_a=True, gate_first=True, div=1.0),
    dict(k_is_b=False, masked=False, low=False, left_a=False, gate_first=True, div=float(N)),
    dict(k_is_b=True, masked=True, low=False, left_a=True, gate_first=False, div=1.0),
    dict(k_is_b=False, masked=False, low=False, left_a=True, gate_first=False, div=1.0),
]

K_CENTER, K_MEAN, K_GROUP, K_IDENT, K_DROP, K_FIRST, K_KEEP, K_ONE, K_END = 0, 128, 256, 384, 512, 640, 768, 769, 770
W_CAT, W_BIAS, W_OUT, W_VEC, W_END = 0, 320, 640, 768, 773
V_NW, V_NB, V_OW, V_OB, V_BO = range(5)


class Sem:

    def __init__(self, handle):
        self.s, self.n = handle, CREDIT


def pipeline(eng, rounds, per, *stages):
    for k in range(per):
        for run, lag in stages:
            if k >= lag:
                run(0, k - lag)
    with eng.Fori(1, rounds) as i:
        for k in range(per):
            for run, lag in stages:
                run(i if k >= lag else i - 1, (k - lag) % per)
    for k in range(max(lag for _, lag in stages)):
        for run, lag in stages:
            if k < lag:
                run(rounds - 1, per + k - lag)


def build(nc, x_in, masks, consts, params, out):
    ctx = ExitStack()
    with ctx:
        def sb(name, shape, dt=F32):
            return ctx.enter_context(nc.sbuf_tensor(name, shape, dt))

        sems = []

        def sem(name):
            s = Sem(ctx.enter_context(nc.semaphore(name)))
            sems.append(s)
            return s

        XT = nc.dram_tensor("XT", [NCH, P, COLS], F32).ap()
        XH = nc.dram_tensor("XH", [NCH, 2, P, COLS], F16).ap()
        XHA = nc.dram_tensor("XHA", [2, P, NT, N // 2, P], F16).ap()
        OS = nc.dram_tensor("OS", [NT, N // 16, 4, P, 256], F32).ap()
        OSL = nc.dram_tensor("OSL", [NT, N // 16, 4, P, 256], BF16).ap()

        LR = sb("LR", [P, NT, C, N])
        LRb = LR[:, :, :, :].rearrange("p t c m -> p (t c m)").bitcast(BF16)[:, 0:NT * C * N] \
            .rearrange("p (t c m) -> p t c m", t=NT, c=C)
        flat = LR[:, :, :, :].rearrange("p t c m -> p (t c m)")

        class Arena:

            def __init__(self, at=0):
                self.at = at

            def take(self, cols):
                v = flat[:, self.at:self.at + cols]
                self.at += cols
                assert self.at <= NT * C * N
                return v

        obuf = [sb(f"obuf{i}", [P, 16 * 256]) for i in range(2)]
        xh_b = [[obuf[h // 2][:, at:at + COLS // 2].bitcast(F16) for at in (h % 2 * COLS, h % 2 * COLS + COLS // 2)]
                for h in range(4)]
        squares = [sb(f"squares{i}", [P, 4 * N]) for i in range(2)]
        rings = [[sb(f"{name}s", [P, 2 * BANK])[:, :], square[:, :]] for name, square in zip(("sig", "msg"), squares)]
        sig, msg = ([v[:, i * 256:(i + 1) * 256].rearrange("p (c m) -> p c m", c=C) for v in ring for i in range(4)]
                    for ring in rings)
        sum1 = sb("sum1", [P, NT, 2 * N])
        sum2 = sb("sum2", [P, NT, 2 * N])
        mask_sb = sb("mask_sb", [P, NT, N])
        kst = sb("kst", [P, K_END])
        prms = [sb(f"prm{i}", [P, W_END]) for i in range(2)]
        whigh = sb("whigh", [P, 320], F16)
        wlow = sb("wlow", [P, 320], F16)
        wogs = [[sb(f"wog{i}{part}", [P, P], F16) for part in range(2)] for i in range(2)]
        cen = sb("cen", [P, P])
        wout_cs = [sb(f"wout_c{i}", [P, P]) for i in range(2)]
        small = sb("small", [P, 16])
        stats = sb("stats", [P, 4 * NCH, 6])
        unscales = [small[:, i:i + 1] for i in (11, 13)]
        bias_cs = [small[:, i:i + 1] for i in (12, 14)]
        ones1 = sb("ones1", [1, P])
        eps1 = sb("eps1", [P, 1])
        epso = sb("epso", [P, 1])
        epsx = sb("epsx", [P, 1])

        banks = [ctx.enter_context(nc.psum_tensor(f"bank{i}", [P, GW], F32)) for i in range(4)]

        def bank(i):
            return banks[i // 2][:, (i % 2) * BANK:(i % 2 + 1) * BANK]

        loaded = [sem(f"loaded{i}") for i in range(2)]
        landed = [sem(f"landed{i}") for i in range(4)]
        loaded_xh = [sem(f"loaded_xh{i}") for i in range(4)]
        loaded_xt = [sem(f"loaded_xt{i}") for i in range(4)]
        stored = [sem(f"stored{i}") for i in range(4)]
        prep = sem("prep")
        step = sem("step")
        enter_paired = sem("enter_paired")
        enter_turned = sem("enter_turned")
        enter_copied = sem("enter_copied")
        enter_counted = sem("enter_counted")
        late_folded = sem("late_folded")
        centered = sem("centered")
        variance = sem("variance")
        squared = sem("squared")
        logged = sem("logged")
        rooted = sem("rooted")
        normed = sem("normed")
        centered_out = sem("centered_out")
        highs_ready = sem("highs_ready")
        lows_ready = sem("lows_ready")
        projected = sem("projected")
        gates_ready = sem("gates_ready")
        gates_masked = sem("gates_masked")
        gate_masked_v = sem("gate_masked_v")
        products_ready = sem("products_ready")
        contracted = sem("contracted")
        copied = sem("copied")
        squares_ready = sem("squares_ready")
        summed = sem("summed")
        sums_cleared = sem("sums_cleared")
        turned = sem("turned")
        gate_projected = sem("gate_projected")
        out_projected = sem("out_projected")
        turned_back = sem("turned_back")
        scaled = sem("scaled")
        gate_ready = sem("gate_ready")
        tokens_ready = sem("tokens_ready")
        mean_off = sem("mean_off")
        mean_off_pool = sem("mean_off_pool")
        gated_ready = sem("gated_ready")
        x_ready = sem("x_ready")
        stats_taken = sem("stats_taken")
        normalized = sem("normalized")
        weights = sem("weights")
        folded = sem("folded")
        tick = sem("tick")

        def advance(*counts):
            for sem_, n in counts:
                sem_.n += n

        K = lambda c, rows=P: kst[0:rows, c:c + P]

        def vector_of(number):
            return lambda i, rows=P: prms[number % 2][0:rows, W_VEC + i:W_VEC + i + 1]

        def load_parameters(sp, number):
            sp.dma_start(prms[number % 2][:, :], params[number]).then_inc(prep.s, 16)
            if LAYERS[number]["masked"]:
                sp.dma_start(mask_sb[:, :, :], masks[number // 2]).then_inc(prep.s, 16)

        with nc.Block() as block:
            @block.sync
            def _(sp):
                for s in sems:
                    sp.sem_inc(s.s, CREDIT)
                sp.dma_start(kst[:, :], consts).then_inc(prep.s, 16)
                load_parameters(sp, 0)
                sp.wait_ge(prep.s, prep.n + 48)

            @block.vector
            def _(dve):
                dve.memset(eps1[:, :], EPS)
                dve.memset(ones1[:, :], 1.0)
                dve.memset(epsx[:, :], EPS / X_SCALE ** 2)
        advance((prep, 48))

        def pair_chunk(dram, ut, vb):
            return dram[bass.ds(8 * ut, 8), :, bass.ds(vb * 256, 256)].rearrange("g p f -> p g f")

        def xh_chunk(n, part, rows, k_is_b):
            if k_is_b:
                return XH[bass.ds(n, 1), part, rows, :].rearrange("o p f -> p (o f)")
            return XHA[part, rows, :, bass.ds(8 * n, 8), :].rearrange("p t j a -> p t (j a)")

        def xh_cols(buf, k_is_b):
            return buf if k_is_b else buf.rearrange("p (t f) -> p t f", t=NT)

        def pair_cols(buf, q):
            return buf.rearrange("p (g f) -> p g f", g=8)[:, :, 64 * q:64 * q + 64]

        def by_b(buf, q):
            return buf.rearrange("p (j g r) -> p g j r", g=8, r=16)[:, :, 4 * q:4 * q + 4, :]

        def by_token_cols(buf, q):
            return pair_cols(buf, q).rearrange("p g (j r) -> p g j r", r=16)

        xt_chunks = [flat[:, (4 + h) * COLS:(5 + h) * COLS] for h in range(2)]

        def load_xt_chunk(sp, n, h, k_is_b):
            if k_is_b:
                sp.dma_start(xt_chunks[h], XT[bass.ds(n, 1), :, :].rearrange("o p f -> p (o f)")) \
                    .then_inc(loaded[h].s, 16)
            else:
                sp.dma_start(xt_chunks[h].rearrange("p (g f) -> p g f", g=16),
                             XT[:, :, bass.ds(n * 128, 128)].rearrange("g p f -> p g f")) \
                    .then_inc(loaded[h].s, 16)

        def load_xh_chunk(sp, n, h, k_is_b):
            for s in range(2):
                for part in range(2):
                    sp.dma_start(xh_cols(xh_b[h][s][C * part:C * part + C, :], k_is_b),
                                 xh_chunk(n, part, slice(C * s, C * s + C), k_is_b)) \
                        .then_inc(landed[h].s, 16)

        def fold(number):
            prm, vec, wog, unscale = prms[number % 2], vector_of(number), wogs[number % 2], unscales[number % 2]
            wout_c, bias_c, late = wout_cs[number % 2], bias_cs[number % 2], not LAYERS[number]["gate_first"]
            w_cat, w_out = prm[0:C, W_CAT:W_CAT + 320], prm[:, W_OUT:W_OUT + P]
            most, scale = small[:, 8:9], small[:, 10:11]
            wfold, bfirst, wout_w = squares[0][0:C, 0:320], squares[0][0:C, 320:448], squares[0][:, 448:576]
            wproj, magnitudes = squares[1][:, 0:320], squares[1][:, 320:640]

            def on_pe(pe):
                pe.wait_ge(folded.s, folded.n + (5 if late else 4))
                pe.matmul(bank(3)[:, 0:320], K(K_DROP, C), wfold, start=True, stop=False)
                pe.matmul(bank(3)[:, 0:320], bfirst, w_cat, start=False, stop=False)
                pe.matmul(bank(3)[:, 0:320], K(K_FIRST, 1), prm[0:1, W_BIAS:W_BIAS + 320],
                          start=False, stop=True).then_inc(weights.s, 1)
                if late:
                    pe.matmul(bank(6)[:, 0:P], K(K_CENTER), wout_w, start=True, stop=True)
                    pe.matmul(bank(7)[:, 0:1], w_out, vec(V_OB), start=True, stop=True).then_inc(late_folded.s, 1)
                pe.wait_ge(weights.s, weights.n + 4)
                pe.transpose(bank(4)[0:1, 0:P], most, K(K_IDENT)).then_inc(weights.s, 1)
                pe.wait_ge(weights.s, weights.n + 6)
                pe.matmul(bank(5)[:, 0:1], ones1[0:1, :], small[0:1, 9:10], start=True, stop=True) \
                    .then_inc(weights.s, 1)

            def on_act(act):
                act.wait_ge(weights.s, weights.n + 2)
                act.activation(magnitudes, wproj, ACT.Abs).then_inc(weights.s, 1)

            def start(dve):
                dve.tensor_scalar(wfold, w_cat, vec(V_NW, C), None, ALU.mult).then_inc(folded.s, 1)
                dve.tensor_scalar(bfirst, K(K_FIRST, C), vec(V_NB, C), None, ALU.mult).then_inc(folded.s, 1)
                dve.memset(wog[0][:, :], 0.0).then_inc(folded.s, 1)
                dve.memset(wog[1][:, :], 0.0).then_inc(folded.s, 1)
                if late:
                    dve.tensor_scalar(wout_w, w_out, vec(V_OW), None, ALU.mult).then_inc(folded.s, 1)

            def copy(dve):
                dve.wait_ge(weights.s, weights.n + 1)
                dve.tensor_copy(wproj, bank(3)[:, 0:320]).then_inc(weights.s, 1)

            def greatest(dve):
                dve.wait_ge(weights.s, weights.n + 3)
                dve.reduce_max(most, magnitudes, mybir.AxisListType.X).then_inc(weights.s, 1)

            def rest(dve):
                if late:
                    dve.wait_ge(late_folded.s, late_folded.n + 1)
                    dve.tensor_copy(wout_c[:, :], bank(6)[:, 0:P]).then_inc(late_folded.s, 1)
                    dve.tensor_tensor(bias_c, bank(7)[:, 0:1], vec(V_BO), ALU.add).then_inc(late_folded.s, 1)
                dve.wait_ge(weights.s, weights.n + 5)
                dve.reduce_max(small[0:1, 9:10], bank(4)[0:1, 0:P], mybir.AxisListType.X).then_inc(weights.s, 1)
                dve.wait_ge(weights.s, weights.n + 7)
                dve.tensor_scalar(most, bank(5)[:, 0:1], 1e-30, 1.0 / W_SCALE, ALU.max, ALU.mult) \
                    .then_inc(weights.s, 1)
                dve.wait_ge(weights.s, weights.n + 8)
                dve.reciprocal(scale, most).then_inc(weights.s, 1)
                dve.wait_ge(weights.s, weights.n + 9)
                dve.tensor_scalar(most, scale, X_SCALE, None, ALU.mult).then_inc(weights.s, 1)
                dve.tensor_scalar(wproj, wproj, scale, None, ALU.mult).then_inc(weights.s, 1)
                dve.wait_ge(weights.s, weights.n + 11)
                dve.reciprocal(unscale, most).then_inc(weights.s, 1)
                dve.tensor_copy(whigh[:, :], wproj).then_inc(weights.s, 1)
                dve.wait_ge(weights.s, weights.n + 13)
                dve.tensor_tensor(wlow[:, :], wproj, whigh[:, :], ALU.subtract).then_inc(weights.s, 1)
                dve.wait_ge(weights.s, weights.n + 14)
                for s in range(2):
                    for part, w in enumerate((whigh, wlow)):
                        dve.tensor_copy(wog[part][C * s:C * s + C, C * s:C * s + C],
                                        w[C * s:C * s + C, 256:320]).then_inc(weights.s, 1)

            return on_pe, on_act, start, copy, greatest, rest

        def advance_fold(number):
            advance((weights, 18), (folded, 4))
            if not LAYERS[number]["gate_first"]:
                advance((folded, 1), (late_folded, 3))

        ar = Arena(6 * COLS)
        e_n = xt_chunks + [ar.take(COLS) for _ in range(2)]
        e_x = [ar.take(COLS) for _ in range(2)]
        e_t = [o[:, 0:COLS] for o in obuf]
        x_nat = x_in.rearrange("o (t a) (s v) c -> t (o a) s (v c)", t=NT, s=2)

        def load_x(sp, h, n=None):
            ut, vb = (0, h) if n is None else n
            sp.dma_start(e_n[h].rearrange("p (s f) -> p s f", s=2),
                         x_nat[ut, :, :, bass.ds(vb * 1024, 1024)]).then_inc(landed[h].s, 16)

        fold_pe, fold_act, fold_start, fold_copy, fold_greatest, fold_rest = fold(0)
        with nc.Block() as block:
            @block.sync
            def _(sp):
                for h in range(4):
                    load_x(sp, h)

            @block.tensor
            def _(pe):
                fold_pe(pe)

            @block.scalar
            def _(act):
                fold_act(act)

            @block.vector
            def _(dve):
                fold_start(dve)
                fold_copy(dve)
                fold_greatest(dve)
                fold_rest(dve)
        advance_fold(0)

        with nc.Block() as block:
            @block.sync
            def _(sp):
                with sp.Fori(1, NCH // 4) as i:
                    for h in range(4):
                        n = 4 * i + h
                        sp.wait_ge(enter_paired.s, enter_paired.n + n - 3)
                        sp.sem_inc(tick.s, 1)
                        load_x(sp, h, (i // 2, n % 8))
                for h in range(2):
                    sp.wait_ge(stored[h].s, stored[h].n + 64)
                for h in range(2):
                    sp.wait_ge(enter_paired.s, enter_paired.n + NCH - 3 + h)
                    load_xt_chunk(sp, h, h, LAYERS[0]["k_is_b"])

            @block.tensor
            def _(pe):
                with pe.Fori(0, NCH // 2) as i:
                    for h in range(2):
                        pe.wait_ge(enter_paired.s, enter_paired.n + 2 * i + h + 1)
                        for q in range(4):
                            b = 4 * h + q
                            pe.wait_ge(enter_copied.s, enter_copied.n + 8 * i + b - 7)
                            for j in range(4):
                                last = pe.transpose(
                                    bank(b).rearrange("p (g j r) -> p g j r", g=8, j=4)[:, :, j, :],
                                    e_x[h][:, (4 * q + j) * P:(4 * q + j + 1) * P], K(K_IDENT))
                            last.then_inc(enter_turned.s, 1)

            @block.scalar
            def _(act):
                with act.Fori(0, NCH // 2) as i:
                    for h in range(2):
                        act.wait_ge(stored[h].s, stored[h].n + 16 * i)
                        act.wait_ge(enter_counted.s, enter_counted.n + 8 * i + 4 * h - 4)
                        for q in range(4):
                            act.wait_ge(enter_turned.s, enter_turned.n + 8 * i + 4 * h + q + 1)
                            act.activation(pair_cols(e_t[h], q),
                                           bank(4 * h + q).rearrange("p (g f) -> p g f", g=8),
                                           ACT.Copy).then_inc(enter_copied.s, 1)
                        act.wait_ge(enter_copied.s, enter_copied.n + 8 * i + 4 * h + 4)
                        ut, vb = i // 4, (2 * i + h) % 8
                        act.dma_start(pair_chunk(XT, ut, vb), e_t[h].rearrange("p (g f) -> p g f", g=8)) \
                            .then_inc(stored[h].s, 16)

            @block.vector
            def _(dve):
                def pair(i, k):
                    if k % 4 == 0:
                        h = k // 4
                        dve.wait_ge(landed[h].s, landed[h].n + 16 * i + 16)
                        dve.wait_ge(enter_turned.s, enter_turned.n + 16 * i + k - 4)
                        dve.tensor_copy(e_x[h % 2].rearrange("p (v s c) -> p s v c", s=2, c=C),
                                        e_n[h].rearrange("p (s v c) -> p s v c", s=2, c=C)) \
                            .then_inc(enter_paired.s, 1)

                def count(i, k):
                    dve.wait_ge(enter_copied.s, enter_copied.n + 16 * i + k + 1)
                    dve.bn_stats(stats[:, bass.ds(16 * i + k, 1), :].rearrange("p o f -> p (o f)"),
                                 pair_cols(e_t[k // 4 % 2], k % 4)).then_inc(enter_counted.s, 1)

                pipeline(dve, NCH // 4, 16, (pair, 0), (count, 4))
        advance(*((landed[h], 4 * NCH) for h in range(4)), (stored[0], 8 * NCH), (stored[1], 8 * NCH),
                (enter_paired, NCH), (enter_turned, 4 * NCH), (enter_copied, 4 * NCH), (enter_counted, 4 * NCH))

        def prepare(number, layer):
            mean, var = small[:, 0:1], small[:, 1:2]
            dev, second, logarithm, a, b, cb = (small[:, i:i + 1] for i in range(2, 8))
            with nc.Block() as block:
                @block.tensor
                def _(pe):
                    pe.wait_ge(step.s, step.n + 1)
                    pe.matmul(bank(0)[:, 0:1], K(K_GROUP), mean, start=True, stop=True).then_inc(step.s, 1)
                    pe.wait_ge(step.s, step.n + 4)
                    pe.matmul(bank(1)[:, 0:1], K(K_GROUP), second, start=True, stop=True).then_inc(step.s, 1)
                    pe.wait_ge(step.s, step.n + 8)
                    pe.matmul(bank(2)[:, 0:1], K(K_CENTER), b, start=True, stop=True).then_inc(step.s, 1)

                @block.scalar
                def _(act):
                    act.preload_act_table_set("natural_log_exp_and_others")
                    act.wait_ge(step.s, step.n + 5)
                    act.activation(logarithm, bank(1)[:, 0:1], ACT.Ln, bias=eps1[:, :]).then_inc(step.s, 1)
                    act.wait_ge(step.s, step.n + 6)
                    act.activation(a, logarithm, ACT.Exp, scale=-0.5).then_inc(step.s, 1)

                @block.vector
                def _(dve):
                    dve.bn_aggr(small[:, 0:2], stats[:, :, :].rearrange("p t f -> p (t f)")).then_inc(step.s, 1)
                    dve.wait_ge(step.s, step.n + 2)
                    dve.tensor_tensor(dev, mean, bank(0)[:, 0:1], ALU.subtract).then_inc(step.s, 1)
                    dve.wait_ge(step.s, step.n + 3)
                    dve.scalar_tensor_tensor(second, dev, dev, var, ALU.mult, ALU.add).then_inc(step.s, 1)
                    dve.wait_ge(step.s, step.n + 7)
                    dve.tensor_scalar(b, bank(0)[:, 0:1], a, -1.0, ALU.mult, ALU.mult).then_inc(step.s, 1)
                    dve.tensor_scalar(cen[:, :], K(K_CENTER), a, None, ALU.mult).then_inc(step.s, 1)
                    dve.wait_ge(step.s, step.n + 10)
                    dve.tensor_copy(cb, bank(2)[:, 0:1]).then_inc(step.s, 1)
            advance((step, 11))

        def norm(block, number, layer):
            ar = Arena(6 * COLS)
            xa = xt_chunks
            high, low = ([ar.take(COLS // 2).bitcast(F16), v[:, :, :].rearrange("p t n -> p (t n)").bitcast(F16)]
                         for v in (sum1, sum2))
            sq, yc, lnv, rs = ([ar.take(GW) for _ in range(k)] for k in (2, 4, 2, 4))
            cb, k_is_b = small[:, 7:8], layer["k_is_b"]
            keep, one = kst[:, K_KEEP:K_KEEP + 1], kst[:, K_ONE:K_ONE + 1]
            @block.sync
            def _(sp):
                def store(n, h):
                    sp.wait_ge(lows_ready.s, lows_ready.n + 2 * n + 2)
                    sp.sem_inc(tick.s, 1)
                    for part, v in enumerate((high[h], low[h])):
                        sp.dma_start(xh_chunk(n, part, slice(0, P), k_is_b), xh_cols(v, k_is_b)) \
                            .then_inc(stored[h].s, 16)

                for h in range(4):
                    sp.wait_ge(stored[h].s, stored[h].n)

                def load_next(i, k):
                    sp.wait_ge(centered.s, centered.n + 4 * i + 2 * k + 2)
                    sp.sem_inc(tick.s, 1)
                    load_xt_chunk(sp, 2 * i + k + 2, k, k_is_b)

                pipeline(sp, NCH // 2 - 1, 2, (load_next, 0), (lambda i, k: store(2 * i + k, k), 1))
                for h in range(2):
                    sp.wait_ge(stored[h].s, stored[h].n + 64)
                load_xh_chunk(sp, 0, 0, k_is_b)
                store(NCH - 2, 0)
                load_xh_chunk(sp, 1, 1, k_is_b)
                store(NCH - 1, 1)

            @block.tensor
            def _(pe):
                def center(i, k):
                    h, t = divmod(k, 2)
                    if t == 0:
                        pe.wait_ge(loaded[h].s, loaded[h].n + 16 * i + 16)
                    pe.wait_ge(centered_out.s, centered_out.n + 4 * i + k - 1)
                    for u in range(2):
                        at = 2 * t + u
                        cols = xa[h][:, at * BANK:(at + 1) * BANK] if k_is_b else \
                            xa[h].rearrange("p (g j r) -> p j g r", g=16, j=8)[
                                :, 4 * (at % 2):4 * (at % 2) + 4, 8 * (at // 2):8 * (at // 2) + 8, :]
                        last = pe.matmul(banks[k % 2][:, u * BANK:(u + 1) * BANK], cen[:, :], cols,
                                         start=True, stop=True)
                    last.then_inc(centered.s, 1)

                def vary(i, k):
                    pe.wait_ge(squared.s, squared.n + 4 * i + k + 1)
                    pe.wait_ge(logged.s, logged.n + 4 * i + k - 1)
                    for u in range(2):
                        last = pe.matmul(banks[2 + k % 2][:, u * BANK:(u + 1) * BANK], K(K_MEAN),
                                         sq[k % 2][:, u * BANK:(u + 1) * BANK], start=True, stop=True)
                    last.then_inc(variance.s, 1)

                pipeline(pe, NCH // 2, 4, (center, 0), (vary, 1))

            @block.scalar
            def _(act):
                def square(i, k):
                    act.wait_ge(centered.s, centered.n + 4 * i + k + 1)
                    act.wait_ge(variance.s, variance.n + 4 * i + k - 1)
                    act.activation(sq[k % 2], banks[k % 2][:, :], ACT.Square, bias=cb).then_inc(squared.s, 1)

                def root(i, k):
                    act.wait_ge(variance.s, variance.n + 4 * i + k + 1)
                    act.wait_ge(rooted.s, rooted.n + 4 * i + k - 1)
                    act.activation(lnv[k % 2], banks[2 + k % 2][:, :], ACT.Ln, bias=epsx[:, :],
                                   scale=1.0 / X_SCALE ** 2).then_inc(logged.s, 1)
                    act.wait_ge(logged.s, logged.n + 4 * i + k + 1)
                    act.wait_ge(normed.s, normed.n + 4 * i + k - 3)
                    act.activation(rs[k], lnv[k % 2], ACT.Exp, scale=-0.5).then_inc(rooted.s, 1)

                pipeline(act, NCH // 2, 4, (square, 0), (root, 1))

            @block.gpsimd
            def _(pool):
                def multiply(i, k):
                    pool.wait_ge(rooted.s, rooted.n + 4 * i + k + 1)
                    pool.wait_ge(centered_out.s, centered_out.n + 4 * i + k + 1)
                    pool.tensor_tensor(yc[k], yc[k], rs[k], ALU.mult).then_inc(normed.s, 1)

                pipeline(pool, NCH // 2, 4, (multiply, 0))

            @block.vector
            def _(dve):
                def copy_out(i, k):
                    dve.wait_ge(squared.s, squared.n + 4 * i + k + 1)
                    dve.wait_ge(lows_ready.s, lows_ready.n + 4 * i + k - 3)
                    dve.tensor_scalar(yc[k], banks[k % 2][:, :], cb, keep, ALU.add, ALU.mult) \
                        .then_inc(centered_out.s, 1)

                def split(i, k):
                    h, cols = k // 2, slice((k % 2) * GW, (k % 2 + 1) * GW)
                    dve.wait_ge(normed.s, normed.n + 4 * i + k + 1)
                    if k % 2 == 0:
                        dve.wait_ge(stored[h].s, stored[h].n + 32 * i)
                    dve.tensor_scalar(high[h][:, cols], yc[k], one, None, ALU.add).then_inc(highs_ready.s, 1)
                    dve.wait_ge(highs_ready.s, highs_ready.n + 4 * i + k + 1)
                    dve.scalar_tensor_tensor(low[h][:, cols], yc[k], one, high[h][:, cols],
                                             ALU.add, ALU.subtract).then_inc(lows_ready.s, 1)

                pipeline(dve, NCH // 2, 4, (copy_out, 0), (split, 2))
            advance((loaded[0], 8 * NCH), (loaded[1], 8 * NCH), (stored[0], 16 * NCH), (stored[1], 16 * NCH),
                    (centered, 2 * NCH), (variance, 2 * NCH), (squared, 2 * NCH), (logged, 2 * NCH),
                    (rooted, 2 * NCH), (normed, 2 * NCH), (centered_out, 2 * NCH), (highs_ready, 2 * NCH),
                    (lows_ready, 2 * NCH))

        def project(block, number, layer, half):
            k_is_b, masked = layer["k_is_b"], layer["masked"]
            dest = LRb if layer["low"] else LR
            gate, unscale = msg if masked else sig, unscales[number % 2]
            by_vector, by_pool = (1, 5), (0, 2, 3, 4, 6, 7)

            def where(n, g):
                if k_is_b:
                    return g // 4, 16 * n + 4 * (g % 4)
                return g // 2 % 2, P * (g // 4) + 8 * n + 4 * (g % 2)

            @block.sync
            def _(sp):
                if half == 1:
                    sp.wait_ge(stored[1].s, stored[1].n)
                    sp.wait_ge(summed.s, summed.n)
                for h in range(2, 4):
                    load_xh_chunk(sp, h, h, k_is_b)
                if half == 0:
                    for h in range(2):
                        sp.wait_ge(stored[h].s, stored[h].n)
                with sp.Fori(1, NCH // 4) as i:
                    for h in range(4):
                        n = 4 * i + h
                        sp.wait_ge(projected.s, projected.n + 8 * n - 24)
                        sp.sem_inc(tick.s, 1)
                        load_xh_chunk(sp, n, h, k_is_b)

            @block.tensor
            def _(pe):
                if half == 0:
                    pe.wait_ge(centered_out.s, centered_out.n)
                    pe.wait_ge(logged.s, logged.n)
                else:
                    pe.wait_ge(copied.s, copied.n)
                with pe.Fori(0, NCH // 4) as i:
                    for h in range(4):
                        pe.wait_ge(landed[h].s, landed[h].n + 64 * i + 64)
                        for g in range(8):
                            pe.wait_ge(products_ready.s, products_ready.n + 32 * i + 8 * h + g - 7)
                            for j in range(4):
                                x = xh_b[h][g // 4]
                                if k_is_b:
                                    tokens = x.rearrange("p (b r) -> p b r", r=16)[:, :, 4 * (g % 4) + j]
                                else:
                                    tokens = x[:, (4 * (g % 4) + j) * P:(4 * (g % 4) + j + 1) * P]
                                for part, w in enumerate((whigh, wlow)):
                                    last = pe.matmul(bank(g)[:, j * P:(j + 1) * P], tokens,
                                                     w[:, half * P:(half + 1) * P], start=part == 0, stop=part == 1)
                            last.then_inc(projected.s, 1)

            @block.scalar
            def _(act):
                if half == 0:
                    act.preload_act_table_set("sigmoid_and_others")
                with act.Fori(0, NCH // 4) as i:
                    for h in range(4):
                        for g in range(8):
                            group = 32 * i + 8 * h + g
                            act.wait_ge(projected.s, projected.n + group + 1)
                            if half == 1 and g >= 4:
                                act.wait_ge(summed.s, summed.n)
                            if not masked:
                                act.wait_ge(products_ready.s, products_ready.n + group - 7)
                            elif g in by_vector:
                                act.wait_ge(gate_masked_v.s, gate_masked_v.n + 2 * (4 * i + h) + by_vector.index(g) - 1)
                            else:
                                act.wait_ge(gates_masked.s, gates_masked.n + 6 * (4 * i + h) + by_pool.index(g) - 5)
                            act.activation(sig[g], bank(g).rearrange("p (m c) -> p c m", m=4)[:, C:, :],
                                           ACT.Sigmoid, scale=unscale).then_inc(gates_ready.s, 1)

            if masked:
                @block.gpsimd
                def _(pool):
                    with pool.Fori(0, NCH // 4) as i:
                        for h in range(4):
                            for g in by_pool:
                                group = 32 * i + 8 * h + g
                                kt, m = where(4 * i + h, g)
                                pool.wait_ge(gates_ready.s, gates_ready.n + group + 1)
                                if half == 1 and g >= 4:
                                    pool.wait_ge(summed.s, summed.n)
                                pool.wait_ge(products_ready.s, products_ready.n + group - 7)
                                pool.tensor_tensor(msg[g], sig[g],
                                                   mask_sb[:, kt, bass.ds(m, 4)].unsqueeze(1).broadcast_to([P, C, 4]),
                                                   ALU.mult).then_inc(gates_masked.s, 1)

            @block.vector
            def _(dve):
                if half == 0:
                    dve.wait_ge(stored[0].s, stored[0].n)
                    dve.wait_ge(lows_ready.s, lows_ready.n)
                with dve.Fori(0, NCH // 4) as i:
                    for h in range(4):
                        for g in range(8):
                            group = 32 * i + 8 * h + g
                            kt, m = where(4 * i + h, g)
                            if masked and g + 1 in by_vector:
                                kt_v, m_v = where(4 * i + h, g + 1)
                                dve.wait_ge(gates_ready.s, gates_ready.n + group + 2)
                                dve.wait_ge(products_ready.s, products_ready.n + group - 6)
                                dve.tensor_tensor(msg[g + 1], sig[g + 1],
                                                  mask_sb[:, kt_v, bass.ds(m_v, 4)].unsqueeze(1).broadcast_to([P, C, 4]),
                                                  ALU.mult).then_inc(gate_masked_v.s, 1)
                            if not masked:
                                dve.wait_ge(gates_ready.s, gates_ready.n + group + 1)
                            elif g in by_vector:
                                dve.wait_ge(gate_masked_v.s, gate_masked_v.n + 2 * (4 * i + h) + by_vector.index(g) + 1)
                            else:
                                dve.wait_ge(gates_masked.s, gates_masked.n + 6 * (4 * i + h) + by_pool.index(g) + 1)
                            dve.scalar_tensor_tensor(dest[:, kt, :, bass.ds(m, 4)],
                                                     bank(g).rearrange("p (m c) -> p c m", m=4)[:, 0:C, :],
                                                     unscale, gate[g], ALU.mult, ALU.mult) \
                                .then_inc(products_ready.s, 1)
            advance(*((landed[h], 16 * NCH) for h in range(4)), (projected, 8 * NCH), (gates_ready, 8 * NCH),
                    (products_ready, 8 * NCH))
            if masked:
                advance((gates_masked, 6 * NCH), (gate_masked_v, 2 * NCH))

        slot = lambda c: flat[:, c * COLS:(c + 1) * COLS]
        fin_xt = [slot(c) for c in (8, 12, 0, 2)]
        fin_xh = [[slot(c)[:, part * COLS // 2:(part + 1) * COLS // 2].bitcast(F16) for part in range(2)]
                  for c in (9, 13, 1, 3)]
        fin_os = [slot(c) for c in (4, 5, 6, 7)]
        fin_low = [o.bitcast(BF16)[:, 0:COLS] for o in fin_os]

        def at(i, h):
            return i // 2, (4 * i + h) % 8

        def tall(v):
            return v.rearrange("p (g f) -> p g f", g=8)

        def load_os(sp, layer, i, h):
            ut, vb = at(i, h)
            buf, dram = (fin_low, OSL) if layer["low"] else (fin_os, OS)
            for s in range(2):
                sp.dma_start(buf[h][:, s * 1024:(s + 1) * 1024].rearrange("p (q f) -> p q f", q=4),
                             dram[bass.ds(ut, 1), bass.ds(8 * s + vb, 1)]
                             .rearrange("t o q p f -> p (t o q) f")).then_inc(landed[h].s, 16)

        def load_xh(sp, layer, i, h):
            ut, vb = at(i, h)
            for part in range(2):
                if layer["k_is_b"]:
                    sp.dma_start(tall(fin_xh[h][part]),
                                 XH[bass.ds(8 * ut, 8), part, :, bass.ds(vb * 256, 256)]
                                 .rearrange("g p f -> p g f")).then_inc(loaded_xh[h].s, 16)
                else:
                    sp.dma_start(fin_xh[h][part].rearrange("p (t f) -> p t f", t=1),
                                 XHA[part, :, bass.ds(ut, 1), bass.ds(16 * vb, 16), :]
                                 .rearrange("p t j a -> p t (j a)")).then_inc(loaded_xh[h].s, 16)

        def load_xt(sp, layer, i, h):
            ut, vb = at(i, h)
            sp.dma_start(tall(fin_xt[h]), pair_chunk(XT, ut, vb)).then_inc(loaded_xt[h].s, 16)

        def contract(block, number, layer, half):
            low = layer["low"]
            src = LRb if low else LR
            off_a, off_b = (0, HALF) if layer["left_a"] else (HALF, 0)
            hold = [(o[:, :].bitcast(BF16)[:, 0:16 * 256] if low else o[:, :]) for o in obuf]
            by_block = [o.rearrange("p (v c r) -> p v c r", v=16, c=16) for o in hold]
            by_channel = [o.rearrange("p (v c r) -> p c v r", v=16, c=16) for o in hold]
            parts = [(piece, g) for piece in range(4) for g in range(4)]
            @block.tensor
            def _(pe):
                pe.wait_ge(products_ready.s, products_ready.n)
                for e, (piece, g) in enumerate(parts):
                    cq, ut = divmod(piece, 2)
                    if e >= 4:
                        pe.wait_ge(copied.s, copied.n + e - 3)
                    for c in range(4):
                        ch = 16 * cq + 4 * g + c
                        for kt in range(NT):
                            last = pe.matmul(banks[e % 4][:, c * N:(c + 1) * N],
                                             src[:, kt, off_a + ch, ut * P:(ut + 1) * P],
                                             src[:, kt, off_b + ch, :], start=kt == 0, stop=kt == NT - 1)
                    last.then_inc(contracted.s, 1)

            @block.scalar
            def _(act):
                for e, (piece, g) in enumerate(parts):
                    if piece >= 2 and g == 0:
                        act.wait_ge(stored[piece % 2].s, stored[piece % 2].n + 16)
                        act.wait_ge(summed.s, summed.n + 4 * 4 * (piece - 1))
                    act.wait_ge(contracted.s, contracted.n + e + 1)
                    act.activation(by_channel[piece % 2][:, 4 * g:4 * g + 4, :, :],
                                   banks[e % 4][:, :].rearrange("p (c v r) -> p c v r", c=4, r=16),
                                   ACT.Copy).then_inc(copied.s, 1)
                    act.wait_ge(copied.s, copied.n + e + 1)
                    if e >= 2:
                        act.wait_ge(summed.s, summed.n + 4 * (e - 1))
                    act.activation(squares[e % 2][:, :].rearrange("p (c v r) -> p c v r", c=4, r=16),
                                   by_channel[piece % 2][:, 4 * g:4 * g + 4, :, :],
                                   ACT.Square).then_inc(squares_ready.s, 1)

            @block.vector
            def _(dve):
                if half == 0:
                    dve.wait_ge(stored[1].s, stored[1].n)
                    dve.memset(sum1[:, :, :], 0.0).then_inc(sums_cleared.s, 1)
                    dve.memset(sum2[:, :, :], 0.0).then_inc(sums_cleared.s, 1)
                    dve.wait_ge(sums_cleared.s, sums_cleared.n + 2)
                for e, (piece, g) in enumerate(parts):
                    ut = piece % 2
                    for two in range(2):
                        if two == 0:
                            dve.wait_ge(copied.s, copied.n + e + 1)
                        if e or two:
                            dve.wait_ge(summed.s, summed.n + 4 * e + 2 * two - 1)
                        dve.tensor_tensor(sum1[:, ut, :].rearrange("p (c v r) -> p c v r", c=2, r=16),
                                          sum1[:, ut, :].rearrange("p (c v r) -> p c v r", c=2, r=16),
                                          by_channel[piece % 2][:, 4 * g + 2 * two:4 * g + 2 * two + 2, :, :],
                                          ALU.add).then_inc(summed.s, 1)
                        if two == 0:
                            dve.wait_ge(squares_ready.s, squares_ready.n + e + 1)
                        if e or two:
                            dve.wait_ge(summed.s, summed.n + 4 * e + 2 * two)
                        dve.tensor_tensor(sum2[:, ut, :], sum2[:, ut, :],
                                          squares[e % 2][:, 2 * two * N:2 * (two + 1) * N],
                                          ALU.add).then_inc(summed.s, 1)

            @block.sync
            def _(sp):
                if half == 1 and number + 1 < len(LAYERS):
                    load_parameters(sp, number + 1)
                for piece in range(4):
                    cq, ut = divmod(piece, 2)
                    if half == 0 and piece == 3:
                        sp.wait_ge(stored[0].s, stored[0].n + 32)
                        sp.wait_ge(summed.s, summed.n + 4 * 4 * 3)
                        for h in range(2):
                            load_xh_chunk(sp, h, h, layer["k_is_b"])
                    if half == 1 and piece >= 2:
                        sp.wait_ge(contracted.s, contracted.n + 8)
                        for h in (0, 1) if piece == 2 else () if low else (2,):
                            load_xh(sp, layer, 0, h)
                            load_xt(sp, layer, 0, h)
                        if piece == 3:
                            sp.wait_ge(stored[0].s, stored[0].n + 32)
                            for h in (0,) if low else (0, 1):
                                load_os(sp, layer, 0, h)
                    sp.wait_ge(copied.s, copied.n + 4 * (piece + 1))
                    sp.dma_start((OSL if low else OS)[ut, :, 2 * half + cq, :, :].rearrange("v p f -> p v f"),
                                 hold[piece % 2].rearrange("p (v f) -> p v f", v=16)) \
                        .then_inc(stored[piece % 2].s, 16)
                sp.wait_ge(stored[0].s, stored[0].n + 32)
                if half == 1 and number + 1 < len(LAYERS):
                    sp.wait_ge(prep.s, prep.n + (32 if LAYERS[number + 1]["masked"] else 16))
            if half == 1 and number + 1 < len(LAYERS):
                advance((prep, 32 if LAYERS[number + 1]["masked"] else 16))
            advance((contracted, 16), (copied, 16), (squares_ready, 16), (summed, 64), (stored[0], 32), (stored[1], 32))
            if half == 0:
                advance((sums_cleared, 2))

        def moments(block, number, layer):
            s1 = [sum1[:, :, i * N:(i + 1) * N] for i in range(2)]
            s2 = [sum2[:, :, i * N:(i + 1) * N] for i in range(2)]
            more = number + 1 < len(LAYERS)
            if more:
                fold_pe, fold_act, fold_start, fold_copy, fold_greatest, fold_rest = fold(number + 1)
            @block.sync
            def _(sp):
                sp.wait_ge(contracted.s, contracted.n)
                for h in range(1 if layer["low"] else 2, 4):
                    load_os(sp, layer, 0, h)
                    if h >= (2 if layer["low"] else 3):
                        load_xh(sp, layer, 0, h)
                        load_xt(sp, layer, 0, h)

            @block.tensor
            def _(pe):
                if more:
                    pe.wait_ge(copied.s, copied.n)
                    fold_pe(pe)

            @block.vector
            def _(dve):
                at = [0]

                def then(ins):
                    at[0] += 1
                    ins.then_inc(step.s, 1)
                    dve.wait_ge(step.s, step.n + at[0])

                if more:
                    dve.wait_ge(prep.s, prep.n)
                    fold_start(dve)
                then(dve.memset(epso[:, :], EPS * layer["div"] ** 2))
                then(dve.tensor_tensor(s1[0], s1[0], s1[1], ALU.add))
                then(dve.tensor_scalar(s1[0], s1[0], 1.0 / C, None, ALU.mult))
                if more:
                    fold_copy(dve)
                then(dve.tensor_tensor(s2[0], s2[0], s2[1], ALU.add))
                then(dve.tensor_tensor(s1[1], s1[0], s1[0], ALU.mult))
                if more:
                    fold_greatest(dve)
                then(dve.scalar_tensor_tensor(s2[0], s2[0], 1.0 / C, s1[1], ALU.mult, ALU.subtract))
                dve.tensor_scalar(s2[0], s2[0], 0.0, None, ALU.max).then_inc(step.s, 1)
                if more:
                    fold_rest(dve)

            @block.scalar
            def _(act):
                act.preload_act_table_set("natural_log_exp_and_others")
                if more:
                    fold_act(act)
                act.wait_ge(step.s, step.n + 7)
                act.activation(s2[1], s2[0], ACT.Ln, bias=epso[:, :]).then_inc(step.s, 1)
                act.wait_ge(step.s, step.n + 8)
                act.activation(s2[0], s2[1], ACT.Exp, scale=-0.5).then_inc(step.s, 1)
            advance((step, 9))
            if more:
                advance_fold(number + 1)

        def finish(number, layer):
            low, gate_first, end = layer["low"], layer["gate_first"], number == len(LAYERS) - 1
            k_is_b = layer["k_is_b"]
            xi, xh, o_f = fin_xt, fin_xh, fin_low if low else fin_os
            nrm = [flat[:, c * COLS:(c + 1) * COLS] for c in (10, 11)]
            gated = [flat[:, 14 * COLS + c * BANK:14 * COLS + (c + 1) * BANK] for c in range(4)]
            stores = [o[:, c * COLS:(c + 1) * COLS] for c in range(2) for o in obuf]
            xo, nat = ([flat[:, 15 * COLS:16 * COLS]], stores) if end else (stores, None)
            depth = len(xo)
            aff, og = ([v[:, c * BANK:(c + 1) * BANK] for v in ring for c in range(2)] for ring in rings)
            o_v = [o.rearrange("p (s c v) -> p s c v", s=2, c=C) for o in o_f]
            n_v = [o.rearrange("p (v s c) -> p s c v", s=2, c=C) for o in nrm]
            vec, wog, unscale, bias_c = vector_of(number), wogs[number % 2], unscales[number % 2], bias_cs[number % 2]
            w_out = prms[number % 2][:, W_OUT:W_OUT + P] if gate_first else wout_cs[number % 2][:, :]
            out_nat = out.rearrange("o (t a) (s v) c -> t (o a) s (v c)", t=NT, s=2)
            fed, taken, aff_used = (gated_ready, x_ready, gated_ready) if gate_first else (scaled, gated_ready, out_projected)
            PO, GL, AL, CL, TB, TBA = (3, 3, 5, 6, 0, 0) if gate_first else (2, 4, 0, 6, 5, 4)
            rounds = NCH // 4

            def token(t, i, k):
                h, q = divmod(k, 4)
                ut, vb = at(i, h)
                v = t[:, bass.ds(ut, 1), 0:N].rearrange("p o (s v) -> p (o s) v", s=2)[:, :, bass.ds(16 * vb + 4 * q, 4)]
                return v.unsqueeze(2).broadcast_to([P, 2, C, 4])

            def tile_of(buffers, k):
                h, q = divmod(k, 4)
                return buffers[h % len(buffers)][:, :, :, 4 * q:4 * q + 4]

            def by_token(v):
                return v.rearrange("p (g j r) -> p g j r", g=8, j=4)

            with nc.Block() as block:
                @block.sync
                def _(sp):
                    def store(i, h):
                        ut, vb = at(i, h)
                        if end:
                            sp.wait_ge(tokens_ready.s, tokens_ready.n + 16 * i + 4 * h + 4)
                            sp.sem_inc(tick.s, 1)
                            sp.dma_start(out_nat[bass.ds(ut, 1), :, :, bass.ds(vb * 1024, 1024)]
                                         .rearrange("t a s f -> a (t s) f"),
                                         nat[h].rearrange("p (s f) -> p s f", s=2)).then_inc(stored[h].s, 16)
                        else:
                            sp.wait_ge(x_ready.s, x_ready.n + 16 * i + 4 * h + 4)
                            sp.sem_inc(tick.s, 1)
                            sp.dma_start(pair_chunk(XT, ut, vb), tall(xo[h])).then_inc(stored[h].s, 16)

                    def next_inputs(i, h):
                        sp.wait_ge(normalized.s, normalized.n + 16 * i + 4 * h + 4)
                        sp.sem_inc(tick.s, 1)
                        load_os(sp, layer, i + 1, h)
                        sp.wait_ge(gate_projected.s, gate_projected.n + 16 * i + 4 * h + 4)
                        sp.sem_inc(tick.s, 1)
                        load_xh(sp, layer, i + 1, h)

                    def next_x(i, h):
                        sp.wait_ge(x_ready.s, x_ready.n + 16 * i + 4 * h + 4)
                        sp.sem_inc(tick.s, 1)
                        load_xt(sp, layer, i + 1, h)
                        store(i, h)

                    sp.wait_ge(stored[1].s, stored[1].n)
                    pipeline(sp, rounds - 1, 4, (next_inputs, 0), (next_x, 1))
                    if not end:
                        for h in range(4):
                            sp.wait_ge(stored[h].s, stored[h].n + 48)
                        for h in range(2):
                            sp.wait_ge(normalized.s, normalized.n + 16 * (rounds - 1) + 4 * h + 4)
                            load_xt_chunk(sp, h, h, LAYERS[number + 1]["k_is_b"])
                    for h in range(4):
                        store(rounds - 1, h)
                    if end:
                        for h in range(4):
                            sp.wait_ge(stored[h].s, stored[h].n + 4 * NCH)

                @block.tensor
                def _(pe):
                    def turn(i, k):
                        h, q = divmod(k, 4)
                        tile = 16 * i + k
                        pe.wait_ge(normalized.s, normalized.n + tile + 1)
                        pe.wait_ge(scaled.s, scaled.n + tile - 1)
                        for j in range(4):
                            last = pe.transpose(by_token(bank(k % 2))[:, :, j, :],
                                                nrm[h % 2][:, (4 * q + j) * P:(4 * q + j + 1) * P], K(K_IDENT))
                        last.then_inc(turned.s, 1)

                    def out_gate(i, k):
                        h, q = divmod(k, 4)
                        if q == 0:
                            pe.wait_ge(loaded_xh[h].s, loaded_xh[h].n + 32 * i + 32)
                        pe.wait_ge(gate_ready.s, gate_ready.n + 16 * i + k - 1)
                        for w, part in ((0, 0), (0, 1), (1, 0)):
                            x = xh[h][part]
                            last = pe.matmul(bank(2 + k % 2), wog[w][:, :], pair_cols(x, q) if k_is_b else by_b(x, q),
                                             start=(w, part) == (0, 0), stop=w == 1)
                        last.then_inc(gate_projected.s, 1)

                    def project_out(i, k):
                        tile = 16 * i + k
                        pe.wait_ge(fed.s, fed.n + tile + 1)
                        pe.wait_ge(taken.s, taken.n + tile - 1)
                        pe.matmul(bank(4 + k % 2), w_out, (gated if gate_first else aff)[k % 4],
                                  start=True, stop=True).then_inc(out_projected.s, 1)

                    def turn_back(i, k):
                        h, q = divmod(k, 4)
                        tile = 16 * i + k
                        pe.wait_ge(x_ready.s, x_ready.n + tile + 1)
                        pe.wait_ge(tokens_ready.s, tokens_ready.n + tile - 1)
                        for j in range(4):
                            last = pe.transpose(bank(6 + k % 2)[:, j * P:(j + 1) * P],
                                                xo[h % depth][:, (4 * q + j) * P:(4 * q + j + 1) * P], K(K_IDENT))
                        last.then_inc(turned_back.s, 1)

                    pipeline(pe, rounds, 16, (turn, 0), (out_gate, 0), (project_out, PO),
                             *([(turn_back, TB)] if end else []))

                @block.scalar
                def _(act):
                    def scale_shift(i, k):
                        tile = 16 * i + k
                        act.wait_ge(turned.s, turned.n + tile + 1)
                        act.wait_ge(aff_used.s, aff_used.n + tile - 3)
                        if gate_first:
                            act.activation(aff[k % 4], bank(k % 2), ACT.Identity, bias=vec(V_OB),
                                           scale=vec(V_OW)).then_inc(scaled.s, 1)
                        else:
                            act.activation(aff[k % 4], bank(k % 2), ACT.Copy).then_inc(scaled.s, 1)

                    def sigmoid(i, k):
                        tile = 16 * i + k
                        act.wait_ge(gate_projected.s, gate_projected.n + tile + 1)
                        act.wait_ge(gated_ready.s, gated_ready.n + tile - 3)
                        act.activation(og[k % 4], bank(2 + k % 2), ACT.Sigmoid, scale=unscale).then_inc(gate_ready.s, 1)

                    def back(i, k):
                        h, q = divmod(k, 4)
                        if q == 0:
                            act.wait_ge(stored[h].s, stored[h].n + 16 * i)
                        act.wait_ge(turned_back.s, turned_back.n + 16 * i + k + 1)
                        act.activation(nat[h].rearrange("p (s v c) -> p v s c", s=2, c=C)[:, 4 * q:4 * q + 4, :, :],
                                       bank(6 + k % 2).rearrange("p (j s c) -> p j s c", j=4, s=2),
                                       ACT.Copy).then_inc(tokens_ready.s, 1)

                    act.preload_act_table_set("sigmoid_and_others")
                    pipeline(act, rounds, 16, (scale_shift, 0), (sigmoid, 0), *([(back, TBA)] if end else []))

                @block.gpsimd
                def _(pool):
                    def normalize(i, k):
                        if k % 4 == 3:
                            pool.wait_ge(landed[k // 4].s, landed[k // 4].n + 32 * i + 32)
                            pool.wait_ge(turned.s, turned.n + 16 * i + k - 7)
                            pool.tensor_tensor(tile_of(n_v, k), tile_of(o_v, k), token(sum1, i, k), ALU.subtract) \
                                .then_inc(mean_off_pool.s, 1)
                            pool.wait_ge(mean_off_pool.s, mean_off_pool.n + 4 * i + k // 4 + 1)
                        else:
                            pool.wait_ge(mean_off.s, mean_off.n + 12 * i + 3 * (k // 4) + k % 4 + 1)
                        pool.tensor_tensor(tile_of(n_v, k), tile_of(n_v, k), token(sum2, i, k), ALU.mult) \
                            .then_inc(normalized.s, 1)

                    def add(i, k):
                        h, q = divmod(k, 4)
                        if q == 0:
                            pool.wait_ge(loaded_xt[h].s, loaded_xt[h].n + 16 * i + 16)
                            if not end:
                                pool.wait_ge(stored[h].s, stored[h].n + 16 * i)
                        if end:
                            pool.wait_ge(turned_back.s, turned_back.n + 16 * i + k - 3)
                        else:
                            pool.wait_ge(stats_taken.s, stats_taken.n + 16 * i + k - 15)
                        pool.wait_ge(gated_ready.s, gated_ready.n + 16 * i + k + 1)
                        pool.tensor_tensor(by_b(xo[h % depth], q) if end else by_token_cols(xo[h % depth], q),
                                           by_token(gated[k % 4]), by_token_cols(xi[h], q),
                                           ALU.add).then_inc(x_ready.s, 1)

                    if gate_first:
                        pipeline(pool, rounds, 16, (normalize, 0))
                    else:
                        pipeline(pool, rounds, 16, (add, 0))

                @block.vector
                def _(dve):
                    def center(i, k):
                        if k % 4 == 3:
                            return
                        if k % 4 == 0:
                            dve.wait_ge(landed[k // 4].s, landed[k // 4].n + 32 * i + 32)
                        dve.wait_ge(turned.s, turned.n + 16 * i + k - 7)
                        dve.tensor_tensor(tile_of(n_v, k), tile_of(o_v, k), token(sum1, i, k), ALU.subtract) \
                            .then_inc(mean_off.s, 1)

                    def normalize(i, k):
                        if k % 4 == 0:
                            dve.wait_ge(landed[k // 4].s, landed[k // 4].n + 32 * i + 32)
                        dve.wait_ge(turned.s, turned.n + 16 * i + k - 7)
                        dve.tensor_tensor(tile_of(n_v, k), tile_of(o_v, k), token(sum2, i, k), ALU.mult) \
                            .then_inc(normalized.s, 1)

                    def gate(i, k):
                        tile = 16 * i + k
                        dve.wait_ge(scaled.s, scaled.n + tile + 1)
                        dve.wait_ge(gate_ready.s, gate_ready.n + tile + 1)
                        dve.wait_ge(out_projected.s, out_projected.n + tile - 3)
                        dve.tensor_tensor(gated[k % 4], aff[k % 4], og[k % 4], ALU.mult).then_inc(gated_ready.s, 1)

                    def add(i, k):
                        h, q = divmod(k, 4)
                        if q == 0:
                            dve.wait_ge(loaded_xt[h].s, loaded_xt[h].n + 16 * i + 16)
                            dve.wait_ge(stored[h].s, stored[h].n + 16 * i)
                        dve.wait_ge(out_projected.s, out_projected.n + 16 * i + k + 1)
                        dve.scalar_tensor_tensor(pair_cols(xo[h % depth], q), tall(bank(4 + k % 2)), vec(V_BO),
                                                 pair_cols(xi[h], q), ALU.add, ALU.add).then_inc(x_ready.s, 1)

                    def gate_late(i, k):
                        tile = 16 * i + k
                        dve.wait_ge(out_projected.s, out_projected.n + tile + 1)
                        dve.wait_ge(gate_ready.s, gate_ready.n + tile + 1)
                        dve.wait_ge(x_ready.s, x_ready.n + tile - 3)
                        dve.scalar_tensor_tensor(gated[k % 4], bank(4 + k % 2), bias_c, og[k % 4],
                                                 ALU.add, ALU.mult).then_inc(gated_ready.s, 1)

                    def count(i, k):
                        h, q = divmod(k, 4)
                        dve.wait_ge(x_ready.s, x_ready.n + 16 * i + k + 1)
                        dve.bn_stats(stats[:, bass.ds(16 * i + k, 1), :].rearrange("p o f -> p (o f)"),
                                     pair_cols(xo[h % depth], q)).then_inc(stats_taken.s, 1)

                    if gate_first:
                        pipeline(dve, rounds, 16, (center, 0), (gate, GL), (add, AL), (count, CL))
                    elif end:
                        pipeline(dve, rounds, 16, (normalize, 0), (gate_late, GL))
                    else:
                        pipeline(dve, rounds, 16, (normalize, 0), (gate_late, GL), (count, CL))
            for h in range(4):
                advance((landed[h], 8 * NCH), (loaded_xh[h], 8 * NCH), (loaded_xt[h], 4 * NCH))
            for h in range(4):
                advance((stored[h], 4 * NCH))
            advance(
                    (turned, 4 * NCH), (gate_projected, 4 * NCH), (out_projected, 4 * NCH), (scaled, 4 * NCH),
                    (gate_ready, 4 * NCH), (gated_ready, 4 * NCH), (x_ready, 4 * NCH), (normalized, 4 * NCH))
            if gate_first:
                advance((mean_off, 3 * NCH), (mean_off_pool, NCH))
            if end:
                advance((turned_back, 4 * NCH), (tokens_ready, 4 * NCH))
            else:
                advance((stats_taken, 4 * NCH))

        for number, layer in enumerate(LAYERS):
            prepare(number, layer)
            with nc.Block() as block:
                norm(block, number, layer)
                for half in range(2):
                    project(block, number, layer, half)
                    contract(block, number, layer, half)
                moments(block, number, layer)
            finish(number, layer)


def constants():
    import numpy as np

    k = np.zeros((P, K_END), np.float32)
    same_half = np.arange(P)[:, None] // C == np.arange(P)[None, :] // C
    channel = np.arange(P) % C
    k[:, K_CENTER:K_CENTER + P] = np.eye(P) - same_half / C
    k[:, K_MEAN:K_MEAN + P] = same_half / C
    k[:, K_GROUP:K_GROUP + P] = (channel[:, None] // 2 == channel[None, :] // 2) / 4
    k[:, K_IDENT:K_IDENT + P] = np.eye(P)
    drop = (channel[:C, None] == channel[None, :]).astype(np.float32)
    drop[0, :] = -1
    drop[:, channel == 0] = 0
    k[:C, K_DROP:K_DROP + P] = drop
    k[:, K_FIRST:K_FIRST + P] = channel[None, :] == 0
    k[:, K_KEEP] = channel != 0
    k[:, K_ONE] = X_SCALE * (channel == 0)
    return k


def pack(wl, wr, wlg, wrg, wog, wo, biases, nw, nb, ow, ob, bo):
    import numpy as np

    p = np.zeros((P, W_END), np.float32)
    order = [(m, h) for h in range(2) for m in range(4)]
    mats, vecs = [wl, wr, wlg, wrg], biases[:4]
    for i, (m, h) in enumerate(order):
        p[:C, W_CAT + 32 * i:W_CAT + 32 * i + 32] = mats[m][:, HALF * h:HALF * h + HALF]
        if vecs[m] is not None:
            p[0, W_BIAS + 32 * i:W_BIAS + 32 * i + 32] = vecs[m][HALF * h:HALF * h + HALF]
    p[:C, W_CAT + 256:W_CAT + 320] = wog
    if biases[4] is not None:
        p[0, W_BIAS + 256:W_BIAS + 320] = biases[4]
    for s in range(2):
        p[C * s:C * s + C, W_OUT + C * s:W_OUT + C * s + C] = wo
        for i, v in enumerate((nw, nb, ow, ob, bo)):
            if v is not None:
                p[C * s:C * s + C, W_VEC + i] = v
    return p


def kernel(**inputs):
    import numpy as np
    import concourse.bacc as bacc
    from concourse.bass_utils import run_bass_kernel_spmd as run

    a = {k: np.asarray(v) for k, v in inputs.items()}
    l0 = {k[8:]: v for k, v in a.items() if k.startswith("L0_conv_")}
    l1 = {k[8:]: v for k, v in a.items() if k.startswith("L1_conv_")}
    l2 = {k[8:]: v for k, v in a.items() if k.startswith("L2_conv_")}
    l3 = {k[8:]: v for k, v in a.items() if k.startswith("L3_conv_")}
    params = np.stack([
        pack(l0["w_left"].T, l0["w_right"].T, l0["w_lgate"].T, l0["w_rgate"].T, l0["w_ogate"].T, l0["w_out"].T,
             [None] * 5, l0["norm_w"], l0["norm_b"], l0["onorm_w"], l0["onorm_b"], None),
        pack(l1["Wl"], l1["Wr"], l1["Wlg"], l1["Wrg"], l1["Wog"], l1["Wo"],
             [l1["bl"], l1["br"], l1["blg"], l1["brg"], l1["bog"]],
             l1["norm_a"], l1["norm_b"], l1["on_a"], l1["on_b"], l1["bo"]),
        pack(l2["w_a_p"], l2["w_b_p"], l2["w_a_g"], l2["w_b_g"], l2["w_g"], l2["w_z"],
             [l2["b_a_p"], l2["b_b_p"], l2["b_a_g"], l2["b_b_g"], l2["b_g"]],
             l2["ln_in_scale"], l2["ln_in_bias"], l2["ln_out_scale"], l2["ln_out_bias"], l2["b_z"]),
        pack(l3["Wl"], l3["Wr"], l3["Wlg"], l3["Wrg"], l3["Wog"], l3["Wo"],
             [l3["bl"], l3["br"], l3["blg"], l3["brg"], l3["bog"]],
             l3["ln_in_g"], l3["ln_in_b"], l3["ln_out_g"], l3["ln_out_b"], l3["bo"]),
    ])
    masks = np.stack([np.ascontiguousarray(m[0].T.reshape(NT, P, N).transpose(1, 0, 2))
                      for m in (l0["mask"], l2["mask"])])
    arrays = {"x": np.ascontiguousarray(a["x"]), "masks": masks, "consts": constants(), "params": params}
    nc = bacc.Bacc("TRN2", target_bir_lowering=False, num_devices=1)
    aps = [nc.dram_tensor(name, v.shape, F32, kind="ExternalInput").ap() for name, v in arrays.items()]
    out = nc.dram_tensor("out", a["x"].shape, F32, kind="ExternalOutput").ap()
    build(nc, *aps, out)
    return run(nc, [arrays], core_ids=[0]).results[0]["out"]
```
